# Optimizing a Trainium2 kernel written in Bass

```python
import numpy as np
import jax
import jax.numpy as jnp

def _softmax(x, axis=-1):
    return jax.nn.softmax(x, axis=axis)

def _gelu(x):
    return jax.nn.gelu(x, approximate=True)

def _silu(x):
    return jax.nn.silu(x)

def _sigmoid(x):
    return jax.nn.sigmoid(x)

def _layernorm(x, axis=-1, eps=1e-05):
    m = jnp.mean(x, axis=axis, keepdims=True)
    v = jnp.var(x, axis=axis, keepdims=True)
    return (x - m) / jnp.sqrt(v + eps)

def _scatter_add(tgt, idx, src, axis=0):
    return tgt.at[idx].add(src)

def _segment_sum(src, seg, n):
    return jax.ops.segment_sum(src, seg, n)
kernel_name = 'mk_flamingo_gated_d1_seqx_r4_667d55'

def setup_inputs(seed: int=0):
    np.random.seed(seed)
    _w = jnp.asarray

    def _rec_inputs():
        import jax
        import jax.numpy as jnp
        _rk = jax.random.key(seed)
        x = -0.0002928 + 1 * jax.random.normal(jax.random.fold_in(_rk, 1), (8, 112, 256), jnp.float32)
        _lenS = 112 - jax.random.randint(jax.random.fold_in(_rk, 7), (8,), 0, max(1, 112 // 4) + 1, jnp.int32)
        _lenS2 = 375 - jax.random.randint(jax.random.fold_in(_rk, 8), (8,), 0, max(1, 375 // 4) + 1, jnp.int32)
        _ctx_1024P = jax.random.normal(jax.random.fold_in(_rk, 11), (8, 16, 256), jnp.float32)
        _ctx_1024c = jax.random.dirichlet(jax.random.fold_in(_rk, 511), 0.3 * jnp.ones((16,), jnp.float32), (8, 375))
        _ctx_1024t = jnp.einsum('bsk,bkd->bsd', _ctx_1024c, _ctx_1024P)
        _ctx_1024t = _ctx_1024t * jax.lax.rsqrt(jnp.mean(jnp.square(_ctx_1024t)) + 1e-12) * 0.953939
        ctx_1024 = -1.39393e-06 + 0.999914 * (_ctx_1024t + 0.3 * jax.random.normal(jax.random.fold_in(_rk, 611), (8, 375, 256), jnp.float32))
        _g = jax.random.normal(jax.random.fold_in(_rk, 9001), (2, 1), jnp.float32)
        _g = jnp.sign(_g) * jnp.maximum(jnp.abs(_g), 1.0) + (_g == 0) * 1.0
        g_xattn = _g[0]
        g_ffn = _g[1]
        return (x, ctx_1024, g_xattn, g_ffn)
    x, ctx_1024, g_xattn, g_ffn = _rec_inputs()

    def _L0_xattn_setup():
        import jax, jax.numpy as jnp
        import numpy as np
        HIDDEN = 256
        HEADS = 16
        HEAD_DIM = HIDDEN // HEADS
        key = jax.random.key(seed)
        ks = jax.random.split(key, 11)
        B, S = (2, 512)
        s = 1.0 / np.sqrt(HIDDEN)
        return {'query': jax.random.normal(ks[0], (B, S, HIDDEN), jnp.float32), 'key': jax.random.normal(ks[1], (B, S, HIDDEN), jnp.float32), 'value': jax.random.normal(ks[2], (B, S, HIDDEN), jnp.float32), 'Wq': jax.random.uniform(ks[3], (HIDDEN, HIDDEN), jnp.float32, -s, s), 'bq': jax.random.uniform(ks[4], (HIDDEN,), jnp.float32, -s, s), 'Wk': jax.random.uniform(ks[5], (HIDDEN, HIDDEN), jnp.float32, -s, s), 'bk': jax.random.uniform(ks[6], (HIDDEN,), jnp.float32, -s, s), 'Wv': jax.random.uniform(ks[7], (HIDDEN, HIDDEN), jnp.float32, -s, s), 'bv': jax.random.uniform(ks[8], (HIDDEN,), jnp.float32, -s, s), 'Wo': jax.random.uniform(ks[9], (HIDDEN, HIDDEN), jnp.float32, -s, s), 'bo': jax.random.uniform(ks[10], (HIDDEN,), jnp.float32, -s, s)}
    _L0_xattn_all = _L0_xattn_setup()
    _L0_xattn_in = {k: v for k, v in _L0_xattn_all.items() if k in ('Wq', 'bq', 'Wk', 'bk', 'Wv', 'bv', 'Wo', 'bo')}
    del _L0_xattn_all

    def _L0_ffn_setup():
        import jax, jax.numpy as jnp
        import numpy as np
        D_MODEL = 256
        FFN = 256
        N_EXPERTS = 8
        N_SHARED = 1
        TOP_K = 2
        B, S = (2, 512)

        def _swiglu(h):
            a, b = jnp.split(h, 2, axis=-1)
            return jax.nn.silu(a) * b
        key = jax.random.key(seed)
        ks = jax.random.split(key, 12)
        sc = 0.02
        return {'x': jax.random.normal(ks[0], (B, S, D_MODEL), dtype=jnp.float32), 'gate_w': jax.random.normal(ks[1], (D_MODEL, N_EXPERTS), dtype=jnp.float32) * sc, 'gate_b': jnp.zeros((N_EXPERTS,), dtype=jnp.float32), 'sw1': jax.random.normal(ks[2], (N_SHARED, D_MODEL, 2 * FFN), dtype=jnp.float32) * sc, 'sb1': jnp.zeros((N_SHARED, 2 * FFN), dtype=jnp.float32), 'sw2': jax.random.normal(ks[3], (N_SHARED, FFN, D_MODEL), dtype=jnp.float32) * sc, 'sb2': jnp.zeros((N_SHARED, D_MODEL), dtype=jnp.float32), 'rw1': jax.random.normal(ks[4], (N_EXPERTS, D_MODEL, 2 * FFN), dtype=jnp.float32) * sc, 'rb1': jnp.zeros((N_EXPERTS, 2 * FFN), dtype=jnp.float32), 'rw2': jax.random.normal(ks[5], (N_EXPERTS, FFN, D_MODEL), dtype=jnp.float32) * sc, 'rb2': jnp.zeros((N_EXPERTS, D_MODEL), dtype=jnp.float32)}
    _L0_ffn_all = _L0_ffn_setup()
    _L0_ffn_in = {k: v for k, v in _L0_ffn_all.items() if k in ('gate_w', 'gate_b', 'sw1', 'sb1', 'sw2', 'sb2', 'rw1', 'rb1', 'rw2', 'rb2')}
    del _L0_ffn_all
    return {'x': x, 'ctx_1024': ctx_1024, 'g_xattn': g_xattn, 'g_ffn': g_ffn, 'L0_xattn_Wq': _L0_xattn_in['Wq'], 'L0_xattn_bq': _L0_xattn_in['bq'], 'L0_xattn_Wk': _L0_xattn_in['Wk'], 'L0_xattn_bk': _L0_xattn_in['bk'], 'L0_xattn_Wv': _L0_xattn_in['Wv'], 'L0_xattn_bv': _L0_xattn_in['bv'], 'L0_xattn_Wo': _L0_xattn_in['Wo'], 'L0_xattn_bo': _L0_xattn_in['bo'], 'L0_ffn_gate_w': _L0_ffn_in['gate_w'], 'L0_ffn_gate_b': _L0_ffn_in['gate_b'], 'L0_ffn_sw1': _L0_ffn_in['sw1'], 'L0_ffn_sb1': _L0_ffn_in['sb1'], 'L0_ffn_sw2': _L0_ffn_in['sw2'], 'L0_ffn_sb2': _L0_ffn_in['sb2'], 'L0_ffn_rw1': _L0_ffn_in['rw1'], 'L0_ffn_rb1': _L0_ffn_in['rb1'], 'L0_ffn_rw2': _L0_ffn_in['rw2'], 'L0_ffn_rb2': _L0_ffn_in['rb2']}

def reference(x, ctx_1024, g_xattn, g_ffn, L0_xattn_Wq, L0_xattn_bq, L0_xattn_Wk, L0_xattn_bk, L0_xattn_Wv, L0_xattn_bv, L0_xattn_Wo, L0_xattn_bo, L0_ffn_gate_w, L0_ffn_gate_b, L0_ffn_sw1, L0_ffn_sb1, L0_ffn_sw2, L0_ffn_sb2, L0_ffn_rw1, L0_ffn_rb1, L0_ffn_rw2, L0_ffn_rb2):
    import jax
    import jax.numpy as jnp

    def _L0_xattn_ref(query, key, value, Wq, bq, Wk, bk, Wv, bv, Wo, bo):
        import jax, jax.numpy as jnp
        import numpy as np
        HIDDEN = 256
        HEADS = 16
        HEAD_DIM = HIDDEN // HEADS
        B, Sq, _ = query.shape
        Sk = key.shape[1]
        Q = (query @ Wq.T + bq).reshape(B, Sq, HEADS, HEAD_DIM).transpose(0, 2, 1, 3)
        K = (key @ Wk.T + bk).reshape(B, Sk, HEADS, HEAD_DIM).transpose(0, 2, 1, 3)
        V = (value @ Wv.T + bv).reshape(B, Sk, HEADS, HEAD_DIM).transpose(0, 2, 1, 3)
        scale = jnp.sqrt(jnp.float32(HEAD_DIM))
        scores = jnp.einsum('bhqd,bhkd->bhqk', Q, K) / scale
        causal = jnp.tril(jnp.ones((Sq, Sk), dtype=bool))
        scores = jnp.where(causal[None, None], scores, -jnp.inf)
        attn = jax.nn.softmax(scores, axis=-1)
        out = jnp.einsum('bhqk,bhkd->bhqd', attn, V)
        out = out.transpose(0, 2, 1, 3).reshape(B, Sq, HIDDEN)
        return out @ Wo.T + bo

    def _L0_ffn_ref(x, gate_w, gate_b, sw1, sb1, sw2, sb2, rw1, rb1, rw2, rb2):
        import jax, jax.numpy as jnp
        import numpy as np
        D_MODEL = 256
        FFN = 256
        N_EXPERTS = 8
        N_SHARED = 1
        TOP_K = 2
        B, S = (2, 512)

        def _swiglu(h):
            a, b = jnp.split(h, 2, axis=-1)
            return jax.nn.silu(a) * b
        hs = jnp.einsum('bsd,ndf->nbsf', x, sw1) + sb1[:, None, None, :]
        shared_out = jnp.einsum('nbsf,nfd->bsd', _swiglu(hs), sw2) + sb2.sum(0)
        probs = jax.nn.softmax(x @ gate_w + gate_b, axis=-1)
        topk_probs, topk_idx = jax.lax.top_k(probs, TOP_K)
        cw = jnp.sum(jax.nn.one_hot(topk_idx, N_EXPERTS, dtype=x.dtype) * topk_probs[..., None], axis=2)
        hr = jnp.einsum('bsd,edf->ebsf', x, rw1) + rb1[:, None, None, :]
        out_e = jnp.einsum('ebsf,efd->ebsd', _swiglu(hr), rw2) + rb2[:, None, None, :]
        routed_out = jnp.einsum('ebsd,bse->bsd', out_e, cw)
        return shared_out + routed_out
    x = x + jnp.tanh(g_xattn[0]) * _L0_xattn_ref(_layernorm(x, axis=-1), ctx_1024, ctx_1024, L0_xattn_Wq, L0_xattn_bq, L0_xattn_Wk, L0_xattn_bk, L0_xattn_Wv, L0_xattn_bv, L0_xattn_Wo, L0_xattn_bo)
    x = x + jnp.tanh(g_ffn[0]) * _L0_ffn_ref(_layernorm(x, axis=-1), L0_ffn_gate_w, L0_ffn_gate_b, L0_ffn_sw1, L0_ffn_sb1, L0_ffn_sw2, L0_ffn_sb2, L0_ffn_rw1, L0_ffn_rb1, L0_ffn_rw2, L0_ffn_rb2)
    return x

_drawn_inputs = setup_inputs


def setup_inputs(seed=0):
    import zlib

    import numpy as np

    out = dict(_drawn_inputs(seed))
    spreads = {'L0_ffn_gate_b': (0.0, 0.572),
     'L0_ffn_sb1': (0.0, 0.8),
     'L0_ffn_sb2': (0.0, 0.457),
     'L0_ffn_rb1': (0.0, 0.8),
     'L0_ffn_rb2': (0.0, 1.021)}
    factors = {'L0_xattn_Wq': 2.88,
     'L0_xattn_bq': 8.0,
     'L0_xattn_Wk': 2.873,
     'L0_xattn_bk': 64.0,
     'L0_xattn_bv': 3.724,
     'L0_ffn_gate_w': 2.792,
     'L0_ffn_sw1': 3.29,
     'L0_ffn_sw2': 3.273,
     'L0_ffn_rw1': 8.0,
     'L0_ffn_rw2': 8.0}
    for name, (base, spread) in spreads.items():
        noise = np.random.default_rng([zlib.crc32(name.encode()), seed]).standard_normal(out[name].shape)
        drawn = base * np.exp(spread * noise) if base else spread * noise
        out[name] = jnp.asarray(drawn.astype(out[name].dtype))
    for name, factor in factors.items():
        out[name] = (out[name] * factor).astype(out[name].dtype)
    return out
```

```python
from contextlib import ExitStack

import concourse.bass as bass
from concourse import mybir

F32 = mybir.dt.float32
F32R = mybir.dt.float32r
ALU = mybir.AluOpType
ACT = mybir.ActivationFunctionType
AX = mybir.AxisListType

B, S, D = 8, 112, 256
HEADS, HD = 16, 16
KC = D // 128
TOK = B * S
HALF = TOK // 2
G = 4
NG = HEADS // G
E = 9
ER = 8
F = 256
PIECES = 3
PW = 512
EPS = 1e-5
NEG = -1e30
LEAST = -3e38
BIAS_ROWS = E * 2 * F // 128
BIAS2_ROWS = E * D // 128


def block_kernel(nc, x, ctxT, wqT, wkT, wvT, woT, bqk, bvo, gates, gate_w, gate_b, w_all, b_all, out):
    with ExitStack() as ctx:
        def sb(name, shape, dt=F32, scope=ctx):
            return scope.enter_context(nc.sbuf_tensor(name, shape, dt))

        def sem(name):
            return ctx.enter_context(nc.semaphore(name))

        x_sb = sb("x_sb", [S, B, D])
        w_hi = sb("w_hi", [128, E * PIECES * PW], F32R)
        w_lo = sb("w_lo", [128, E * PIECES * PW], F32R)
        ident = sb("ident", [128, 128])
        ones_r = sb("ones_r", [128, 128], F32R)
        gate_cols = sb("gate_cols", [128, 2])
        tanh_gate = sb("tanh_gate", [128, 2])
        stats = sb("stats", [S, B, 6])
        meanvar = sb("meanvar", [S, B, 2])
        std = sb("std", [S, B])
        rstd = sb("rstd", [S, B])

        att = ctx.enter_context(ExitStack())
        ctxT_sb = sb("ctxT_sb", [128, KC, TOK], scope=att)
        xhatT = sb("xhatT", [128, KC, TOK], scope=att)
        wq_sb = sb("wq_sb", [128, KC, D], scope=att)
        wk_sb = sb("wk_sb", [128, KC, D], scope=att)
        wv_sb = sb("wv_sb", [128, KC, D], scope=att)
        wo_sb = sb("wo_sb", [128, KC, D], scope=att)
        bqk_sb = sb("bqk_sb", [128, 2, KC], scope=att)
        bvo_sb = sb("bvo_sb", [S, 2, D], scope=att)
        qT = sb("qT", [128, KC, TOK], scope=att)
        kT = sb("kT", [128, KC, TOK], scope=att)
        v_sb = sb("v_sb", [S, B, D], scope=att)
        mask = sb("mask", [S, S], scope=att)
        q_now = sb("q_now", [128, KC, S], scope=att)
        k_diag = sb("k_diag", [128, NG, G, 2, S], scope=att)
        v_pad = sb("v_pad", [S, HEADS // 2, 2, 2, HD], scope=att)
        raw = sb("raw", [128, PIECES, PW], scope=att)
        sc_sb = sb("sc_sb", [S, 2, G, S], scope=att)
        rowmax = sb("rowmax", [S, 2, G], scope=att)
        pT_sb = sb("pT_sb", [S, 2, G, S], scope=att)
        sums = sb("sums", [S, HEADS], scope=att)
        rsum = sb("rsum", [S, HEADS], scope=att)
        rexp = sb("rexp", [S, HEADS, HD], scope=att)
        rT_sb = sb("rT_sb", [128, KC, S], scope=att)
        oT_sb = sb("oT_sb", [128, KC, S], scope=att)
        y_sb = sb("y_sb", [S, D], scope=att)
        early = att.enter_context(ExitStack())
        xhat = sb("xhat", [S, B, D], scope=early)
        early.close()
        probs = sb("probs", [S, NG, G, S], scope=att)
        att.close()

        x2n = sb("x2n", [S, B, D])
        x2T = sb("x2T", [128, KC, TOK])
        x2T_hi = sb("x2T_hi", [128, KC, TOK], F32R)
        x2T_lo = sb("x2T_lo", [128, KC, TOK], F32R)
        gw_sb = sb("gw_sb", [128, KC, ER])
        gb_sb = sb("gb_sb", [S, ER])
        b_rows = sb("b_rows", [BIAS_ROWS + BIAS2_ROWS, 128])
        b_rows_hi = sb("b_rows_hi", [BIAS_ROWS + BIAS2_ROWS, 128], F32R)
        b_rows_lo = sb("b_rows_lo", [BIAS_ROWS + BIAS2_ROWS, 128], F32R)
        bias = sb("bias", [128, E * (2 * F + D)], F32R)
        pg = sb("pg", [S, B, ER])
        pg2 = sb("pg2", [S, B, ER])
        top = sb("top", [S, 2, B])
        gsum = sb("gsum", [S, B])
        eq = sb("eq", [S, B, ER])
        first = sb("first", [S, B])
        hot = sb("hot", [S, 2, B, ER])
        iota8 = sb("iota8", [S, B, ER])
        cw = sb("cw", [S, B, E])
        acc = sb("acc", [S, B, D])
        th = sb("th", [S, 2, F])
        ug = sb("ug", [S, 2, F])
        gg = sb("gg", [S, 2, F])
        gT_hi = sb("gT_hi", [128, 2, 2, S], F32R)
        gT_lo = sb("gT_lo", [128, 2, 2, S], F32R)

        bank = [ctx.enter_context(nc.psum_tensor(f"bank{n}", [128, 512], F32)) for n in range(8)]

        def grid(t, p, n, w):
            return t[0:p, 0:n * w].rearrange("p (n w) -> p n w", n=n)

        sc_ps = [grid(bank[n], S, G, S) for n in (0, 1)]
        pT_ps = [grid(bank[n], S, G, S) for n in (2, 3)]
        oT_ps = grid(bank[4], 128, KC, S)
        rT_ps = grid(bank[5], 128, KC, S)
        y_ps = bank[6][0:S, 0:D]
        h_ps = [bank[n] for n in (0, 1)]
        gT_ps = [grid(bank[n], 128, 2, S) for n in (2, 3)]
        ye_ps = [bank[n] for n in (4, 5)]
        lg_ps = grid(bank[6], S, B, ER)

        s_wk, s_wv, s_wq, s_small, s_b, s_wo = (
            sem(n) for n in ("wk_in", "wv_in", "wq_in", "small_in", "biases_in", "wo_in"))
        s_x = [sem(f"x_in{n}") for n in range(2)]
        s_ctx = [sem(f"ctx_in{n}") for n in range(2)]
        s_raw = [sem(f"raw_in{j}") for j in range(PIECES)]
        s_const, s_zero = sem("consts_ready"), sem("zeros_ready")
        s_k, s_kt = sem("k_projected"), sem("kT_ready")
        s_v, s_vs = sem("v_projected"), sem("v_ready")
        s_st2, s_x2hi = sem("meanvars_ready"), sem("x2T_hi_ready")
        s_st, s_stats, s_std, s_rstd, s_xh = (
            sem("stats_ready"), sem("meanvar_ready"), sem("std_ready"), sem("rstd_ready"), sem("xhat_ready"))
        s_xt, s_xts = sem("xhat_transposed"), sem("xhatT_ready")
        s_q, s_qt = sem("q_projected"), sem("qT_ready")
        s_tg = sem("tanh_gate_ready")
        s_qn = sem("q_now_ready")
        s_vp = sem("v_pad_ready")
        s_kd = [sem(f"k_diag_in{g}") for g in range(NG)]
        s_sc, s_mk, s_sh, s_ex, s_sum = (
            sem("scores_ready"), sem("scores_masked"), sem("scores_shifted"),
            sem("probs_ready"), sem("sums_ready"))
        s_pt, s_pts, s_pv = sem("probs_transposed"), sem("pT_ready"), sem("pv_done")
        s_rs, s_re, s_rt, s_rts = (
            sem("rsum_ready"), sem("rexp_ready"), sem("rsum_transposed"), sem("rT_ready"))
        s_on, s_y, s_yb, s_x2 = sem("oT_ready"), sem("y_projected"), sem("y_biased"), sem("x2_ready")
        s_whi, s_wlo = sem("w_hi_ready"), sem("w_lo_ready")
        s_brow, s_bias = sem("bias_rows_split"), sem("bias_in")
        s_gl = sem("gate_in")
        s_chain = sem("router_step")
        s_x2t, s_x2ts, s_x2lo = sem("x2n_transposed"), sem("x2T_ready"), sem("x2T_lo_ready")
        s_lg, s_cw = sem("logits_ready"), sem("weights_ready")
        s_gexp = sem("gate_exp_ready")
        s_h, s_th, s_ug, s_gg, s_gt, s_gth, s_gtl, s_ye, s_acc = (
            sem("h_ready"), sem("tanh_ready"), sem("u_ready"), sem("g_ready"), sem("g_transposed"),
            sem("gT_hi_ready"), sem("gT_lo_ready"), sem("ye_ready"), sem("acc_ready"))
        s_fin, s_out = sem("out_ready"), sem("out_stored")

        block = ctx.enter_context(nc.Block())

        def head_rows(h):
            return slice(HD * (h % 8), HD * (h % 8) + HD)

        @block.sync
        def _(sp):
            for n in range(2):
                sp.dma_start(x_sb[:, n * B // 2:(n + 1) * B // 2, :], x[:, n * B // 2:(n + 1) * B // 2, :])\
                    .then_inc(s_x[n], 16)
            sp.dma_start(bqk_sb[:, :, :], bqk).then_inc(s_small, 16)
            sp.dma_start(bvo_sb[:, :, :], bvo.partition_broadcast(S)).then_inc(s_small, 16)
            sp.dma_start(gate_cols[:, :], gates.partition_broadcast(128)).then_inc(s_small, 16)
            sp.dma_start(wv_sb[:, :, :], wvT).then_inc(s_wv, 16)
            sp.dma_start(wq_sb[:, :, :], wqT).then_inc(s_wq, 16)
            sp.dma_start(wo_sb[:, :, :], woT).then_inc(s_wo, 16)
            for j in range(PIECES):
                sp.dma_start(raw[:, j, :], w_all[j]).then_inc(s_raw[j], 16)

            def load_keys(p, g):
                for h in range(G * g, G * g + G):
                    sp.dma_start(k_diag[head_rows(h), g, h % G, :, :],
                                 kT[head_rows(h), h // 8, bass.ds(p * (2 * S), 2 * S)]).then_inc(s_kd[g], 16)

            sp.wait_ge(s_zero, 1)
            sp.wait_ge(s_kt, 2 * KC)
            for g in range(NG):
                load_keys(0, g)
            def load_weights(e, j):
                sp.wait_ge(s_wlo, PIECES * (e - 1) + j + 1)
                sp.dma_start(raw[:, j, :], w_all[bass.ds(PIECES * e + j, 1)].rearrange("a p n -> (a p) n"))\
                    .then_inc(s_raw[j], 16)

            with sp.Fori(0, B // 2 - 1) as p:
                for j in range(PIECES):
                    load_weights(2 * p + 1, j)
                for g in range(NG):
                    sp.wait_ge(s_sc, NG * (2 * p + 1) + g + 1)
                    load_keys(p + 1, g)
                    if g:
                        load_weights(2 * p + 2, g - 1)
            for e in (B - 1, B):
                for j in range(PIECES):
                    load_weights(e, j)
            sp.wait_ge(s_x2, B)
            sp.wait_ge(s_wlo, PIECES * E)
            sp.dma_start(b_rows[:, :], b_all).then_inc(s_b, 16)
            sp.dma_start(gw_sb[:, :, :], gate_w).then_inc(s_gl, 16)
            sp.dma_start(gb_sb[:, :], gate_b.partition_broadcast(S)).then_inc(s_gl, 16)
            sp.wait_ge(s_brow, 2)
            sp.wait_ge(s_zero, 2)
            sp.dma_start(bias[0:1, :].bitcast(F32), b_rows_hi[:, :].bitcast(F32)).then_inc(s_bias, 16)
            sp.dma_start(bias[1:2, :].bitcast(F32), b_rows_lo[:, :].bitcast(F32)).then_inc(s_bias, 16)
            for b in range(B):
                sp.wait_ge(s_fin, b + 1)
                sp.dma_start(out[b], x2n[:, b, :]).then_inc(s_out, 16)
            sp.wait_ge(s_out, 16 * B)

        @block.gpsimd
        def _(pool):
            nc.gpsimd.memset(ident[:, :], 0.0).then_inc(s_const, 1)
            nc.gpsimd.memset(mask[:, :], 0.0).then_inc(s_const, 1)
            pool.wait_ge(s_const, 2)
            nc.gpsimd.affine_select(out=ident[:, :], in_=ident[:, :], compare_op=ALU.not_equal, fill=1.0,
                                    base=0, pattern=[[-1, 128]], channel_multiplier=1).then_inc(s_const, 1)
            nc.gpsimd.affine_select(out=mask[:, :], in_=mask[:, :], compare_op=ALU.is_ge, fill=NEG,
                                    base=0, pattern=[[-1, S]], channel_multiplier=1).then_inc(s_const, 1)
            nc.gpsimd.memset(k_diag[:, :, :, :, :], 0.0).then_inc(s_zero, 1)
            nc.gpsimd.memset(v_pad[:, :, :, :, :], 0.0).then_inc(s_const, 1)
            nc.gpsimd.memset(ones_r[:, :].bitcast(F32), 1.0).then_inc(s_const, 1)

            def split(e, j):
                    at = bass.ds(PW * (PIECES * e + j), PW)
                    pool.wait_ge(s_whi, PIECES * e + j + 1)
                    nc.gpsimd.tensor_tensor(w_lo[:, at], raw[:, j, :], w_hi[:, at], ALU.subtract)\
                        .then_inc(s_wlo, 1)

            def shift(b, g):
                pool.wait_ge(s_mk, NG * b + g + 1)
                nc.gpsimd.tensor_tensor(sc_sb[:, g % 2, :, :], sc_sb[:, g % 2, :, :],
                                        rowmax[:, g % 2, :].unsqueeze(2).to_broadcast([S, G, S]), ALU.subtract)\
                    .then_inc(s_sh, 1)

            with pool.Fori(0, B) as b:
                for g in range(NG):
                    shift(b, g)
                    if g:
                        split(b, g - 1)
            for j in range(PIECES):
                split(E - 1, j)
            pool.wait_ge(s_wlo, PIECES * E)
            pool.wait_ge(s_x2, B)
            nc.gpsimd.memset(bias[:, :].bitcast(F32), 0.0).then_inc(s_zero, 1)
            nc.gpsimd.iota(iota8[:, :, :], pattern=[[0, B], [1, ER]], base=0, channel_multiplier=0,
                           allow_small_or_imprecise_dtypes=True).then_inc(s_const, 1)
            nc.gpsimd.memset(acc[:, :, :], 0.0).then_inc(s_const, 1)
            nc.gpsimd.memset(cw[:, :, ER:E], 1.0).then_inc(s_const, 1)

        N_CONST_ATT, N_CONST = 6, 9

        @block.tensor
        def _(pe):
            def project(ps, w, rhs, m, n):
                for k in range(KC):
                    last = nc.tensor.matmul(ps[:, 0:HALF], w[:, k, m * 128:(m + 1) * 128],
                                            rhs[:, k, n * HALF:(n + 1) * HALF], start=(k == 0), stop=(k == KC - 1))
                return last

            pe.wait_ge(s_wk, 16)
            for n in range(2):
                pe.wait_ge(s_ctx[n], 16)
                for m in range(KC):
                    project(bank[2 * n + m], wk_sb, ctxT_sb, m, n).then_inc(s_k, 1)
            def values(p):
                if p >= 2:
                    pe.wait_ge(s_vs, p - 1)
                for b in (2 * p, 2 * p + 1):
                    for k in range(KC):
                        mm = nc.tensor.matmul(bank[6 + p % 2][0:S, (b % 2) * D:(b % 2 + 1) * D],
                                              ctxT_sb[:, k, b * S:(b + 1) * S], wv_sb[:, k, :],
                                              start=(k == 0), stop=(k == KC - 1))
                mm.then_inc(s_v, 1)

            pe.wait_ge(s_wv, 16)
            values(0)
            values(1)
            pe.wait_ge(s_const, 3)
            for n in range(2):
                for b in range(4 * n, 4 * n + 4):
                    pe.wait_ge(s_xh, b + 1)
                    for k in range(KC):
                        t = 2 * n + k
                        if b == 4 * n:
                            pe.wait_ge(s_kt, t + 1)
                        mm = nc.tensor.transpose(bank[t][:, (b % 4) * S:(b % 4 + 1) * S],
                                                 xhat[:, b, k * 128:(k + 1) * 128], ident[0:S, 0:S])
                mm.then_inc(s_xt, 1)
            pe.wait_ge(s_wq, 16)
            for n in range(2):
                pe.wait_ge(s_xts, KC * (n + 1))
                for m in range(KC):
                    if n:
                        pe.wait_ge(s_qt, m + 1)
                    project(bank[4 + m], wq_sb, xhatT, m, n).then_inc(s_q, 1)
            values(2)
            values(3)

            def scores(b, g, first):
                if g == 0:
                    pe.wait_ge(s_qn, b + 1)
                pe.wait_ge(s_kd[g], 16 * G * (b // 2 + 1))
                if not (first and g < 2):
                    pe.wait_ge(s_mk, NG * b + g - 1)
                nc.tensor.matmul(sc_ps[g % 2], q_now[:, g // 2, :],
                                 k_diag[:, g, :, bass.ds(b % 2, 1), :].rearrange("p h o s -> p h (o s)"),
                                 start=True, stop=True).then_inc(s_sc, 1)

            def turn(b, g, first):
                pe.wait_ge(s_ex, NG * b + g + 1)
                if not (first and g < 2):
                    pe.wait_ge(s_pts, NG * b + g - 1)
                for h in range(G):
                    mm = nc.tensor.transpose(pT_ps[g % 2][:, h, :], probs[:, g, h, :], ident[0:S, 0:S])
                mm.then_inc(s_pt, 1)

            def pv(b, g, first):
                pe.wait_ge(s_pts, NG * b + g + 1)
                if g == 0:
                    pe.wait_ge(s_vp, b + 1)
                    if not first:
                        pe.wait_ge(s_on, b)
                for h in range(G):
                    pair = 2 * g + h // 2
                    at = 32 * (pair % 4)
                    mm = nc.tensor.matmul(oT_ps[at:at + 32, g // 2, :],
                                          v_pad[:, pair, h % 2, :, :].rearrange("p a d -> p (a d)"),
                                          pT_sb[:, g % 2, h, :], start=(h % 2 == 0), stop=(h % 2 == 1))
                mm.then_inc(s_pv, 1)

            def turn_rsum(b, first):
                pe.wait_ge(s_re, b + 1)
                if not first:
                    pe.wait_ge(s_rts, b)
                for k in range(KC):
                    mm = nc.tensor.transpose(rT_ps[:, k, :],
                                             rexp[:, 8 * k:8 * k + 8, :].rearrange("p a d -> p (a d)"),
                                             ident[0:S, 0:S])
                mm.then_inc(s_rt, 1)

            def out_proj(b, first):
                pe.wait_ge(s_on, b + 1)
                if first:
                    pe.wait_ge(s_wo, 16)
                    pe.wait_ge(s_vs, B // 2)
                else:
                    pe.wait_ge(s_yb, b)
                for k in range(KC):
                    mm = nc.tensor.matmul(y_ps, oT_sb[:, k, :], wo_sb[:, k, :], start=(k == 0), stop=(k == KC - 1))
                mm.then_inc(s_y, 1)

            def attend(i, now=True, before=True, last=True, first=False, second=False, third=False):
                for g in range(NG):
                    if now:
                        scores(i, g, first)
                    if last and g == 1:
                        out_proj(i - 2, third)
                    if before:
                        turn(i - 1, g, second)
                        if g:
                            pv(i - 1, g - 1, second)
                if before:
                    turn_rsum(i - 1, second)
                    pv(i - 1, NG - 1, second)

            attend(0, before=False, last=False, first=True)
            attend(1, last=False, second=True)
            attend(2, third=True)
            with pe.Fori(3, B) as i:
                attend(i)
            attend(B, now=False)
            out_proj(B - 1, False)

            for n in range(2):
                for b in range(4 * n, 4 * n + 4):
                    pe.wait_ge(s_xh, B + b + 1)
                    for k in range(KC):
                        mm = nc.tensor.transpose(bank[2 * n + k][:, (b % 4) * S:(b % 4 + 1) * S],
                                                 x2n[:, b, k * 128:(k + 1) * 128], ident[0:S, 0:S])
                mm.then_inc(s_x2t, 1)
            pe.wait_ge(s_gl, 32)
            for b in range(B):
                pe.wait_ge(s_x2ts, KC * (b // 4 + 1))
                for k in range(KC):
                    mm = nc.tensor.matmul(lg_ps[:, b, :], x2T[:, k, b * S:(b + 1) * S], gw_sb[:, k, :],
                                          start=(k == 0), stop=(k == KC - 1))
            mm.then_inc(s_lg, 1)

            def split_product(ps, parts_hi, parts_lo, col, width, bias_at):
                nc.tensor.matmul(ps, ones_r[:, 0:S], bias[:, bass.ds(bias_at, width)], start=True, stop=False)
                for k in range(KC):
                    rh = w_hi[:, bass.ds(col + k * width, width)]
                    rl = w_lo[:, bass.ds(col + k * width, width)]
                    nc.tensor.matmul(ps, parts_hi[k], rh, start=False, stop=False)
                    nc.tensor.matmul(ps, parts_hi[k], rl, start=False, stop=False)
                    mm = nc.tensor.matmul(ps, parts_lo[k], rh, start=False, stop=(k == KC - 1))
                return mm

            def up(e, b, first):
                if not (first and b < 2):
                    pe.wait_ge(s_gg, B * e + b - 1)
                t = slice(b * S, (b + 1) * S)
                split_product(h_ps[b % 2][0:S, :], [x2T_hi[:, k, t] for k in range(KC)],
                              [x2T_lo[:, k, t] for k in range(KC)],
                              e * (PIECES * PW), 2 * F, e * (2 * F)).then_inc(s_h, 1)

            def turn_g(e, b, first):
                pe.wait_ge(s_gg, B * e + b + 1)
                if not (first and b < 2):
                    pe.wait_ge(s_gtl, B * e + b - 1)
                for k in range(2):
                    mm = nc.tensor.transpose(gT_ps[b % 2][:, k, :], gg[:, b % 2, k * 128:(k + 1) * 128],
                                             ident[0:S, 0:S])
                mm.then_inc(s_gt, 1)

            def down(e, b, first):
                pe.wait_ge(s_gtl, B * e + b + 1)
                if not (first and b < 2):
                    pe.wait_ge(s_acc, B * e + b - 1)
                split_product(ye_ps[b % 2][0:S, 0:D], [gT_hi[:, b % 2, k, :] for k in range(2)],
                              [gT_lo[:, b % 2, k, :] for k in range(2)],
                              e * (PIECES * PW) + 2 * PW, D, E * 2 * F + e * D).then_inc(s_ye, 1)

            def expert(e, first):
                for b in range(B):
                    up(e, b, first)
                    if not first or b >= 1:
                        turn_g(*((e, b - 1) if b >= 1 else (e - 1, B - 1)), first)
                    if not first or b >= 2:
                        down(*((e, b - 2) if b >= 2 else (e - 1, B - 2 + b)), first)

            pe.wait_ge(s_wlo, PIECES * E)
            pe.wait_ge(s_bias, 32)
            pe.wait_ge(s_x2lo, 4)
            pe.wait_ge(s_const, N_CONST)
            expert(0, True)
            with pe.Fori(1, E) as e:
                expert(e, False)
            turn_g(E - 1, B - 1, False)
            down(E - 1, B - 2, False)
            down(E - 1, B - 1, False)

        @block.scalar
        def _(act):
            act.dma_start(wk_sb[:, :, :], wkT).then_inc(s_wk, 16)
            for n in range(2):
                act.dma_start(ctxT_sb[:, :, n * HALF:(n + 1) * HALF], ctxT[:, :, n * HALF:(n + 1) * HALF])\
                    .then_inc(s_ctx[n], 16)
            nc.scalar.preload_act_table(ACT.Sqrt)
            act.wait_ge(s_small, 48)
            for n in range(2):
                for m in range(KC):
                    t = 2 * n + m
                    act.wait_ge(s_k, t + 1)
                    nc.scalar.activation(kT[:, m, n * HALF:(n + 1) * HALF], bank[t][:, 0:HALF], ACT.Identity,
                                         bias=bqk_sb[:, 1, m:m + 1]).then_inc(s_kt, 1)
            act.wait_ge(s_stats, 1)
            nc.scalar.activation(std[:, :], std[:, :], ACT.Sqrt).then_inc(s_std, 1)
            nc.scalar.activation(tanh_gate[:, :], gate_cols[:, :], ACT.Tanh).then_inc(s_tg, 1)
            for n in range(2):
                act.wait_ge(s_xt, n + 1)
                for k in range(KC):
                    nc.scalar.activation(xhatT[:, k, n * HALF:(n + 1) * HALF], bank[2 * n + k][:, 0:HALF],
                                         ACT.Copy).then_inc(s_xts, 1)
            for n in range(2):
                for m in range(KC):
                    act.wait_ge(s_q, 2 * n + m + 1)
                    nc.scalar.activation(qT[:, m, n * HALF:(n + 1) * HALF], bank[4 + m][:, 0:HALF], ACT.Identity,
                                         bias=bqk_sb[:, 0, m:m + 1]).then_inc(s_qt, 1)

            def take_queries(b):
                nc.scalar.activation(q_now[:, :, :], qT[:, :, bass.ds(b * S, S)], ACT.Copy).then_inc(s_qn, 1)

            def take_values(b):
                for par in range(2):
                    ins = nc.scalar.activation(
                        v_pad[:, :, par, par, :],
                        v_sb[:, bass.ds(b, 1), :].rearrange("p o (a q d) -> p (o a) q d", q=2, d=HD)[:, :, par, :],
                        ACT.Copy)
                ins.then_inc(s_vp, 1)

            def exps(b, g, first):
                act.wait_ge(s_sh, NG * b + g + 1)
                if not first:
                    act.wait_ge(s_pt, NG * (b - 1) + g + 1)
                    act.wait_ge(s_sum, NG * (b - 1) + g + 1)
                nc.scalar.activation(probs[:, g, :, :], sc_sb[:, g % 2, :, :], ACT.Exp, scale=HD ** -0.5)\
                    .then_inc(s_ex, 1)

            def take_pT(b, g, first):
                act.wait_ge(s_pt, NG * b + g + 1)
                if not (first and g < 2):
                    act.wait_ge(s_pv, NG * b + g - 1)
                nc.scalar.activation(pT_sb[:, g % 2, :, :], pT_ps[g % 2], ACT.Copy).then_inc(s_pts, 1)

            def round_weights(e, j):
                act.wait_ge(s_raw[j], 16 * (e + 1))
                nc.scalar.activation(w_hi[:, bass.ds(PW * (PIECES * e + j), PW)], raw[:, j, :], ACT.Copy)\
                    .then_inc(s_whi, 1)

            def take_rT(b, first):
                act.wait_ge(s_rt, b + 1)
                if not first:
                    act.wait_ge(s_on, b)
                nc.scalar.activation(rT_sb[:, :, :], rT_ps, ACT.Copy).then_inc(s_rts, 1)

            def attend(i, now=True, before=True, more=True, first=False, second=False):
                for g in range(NG):
                    if before:
                        take_pT(i - 1, g, second)
                    if g == NG - 1:
                        if before:
                            take_rT(i - 1, second)
                        if more:
                            act.wait_ge(s_sc, NG * i + NG)
                            take_queries(i + 1)
                    if now:
                        exps(i, g, first)
                    if g < PIECES:
                        round_weights(i, g)
                if before:
                    act.wait_ge(s_pv, NG * i)
                if now:
                    take_values(i)

            act.wait_ge(s_qt, 2 * KC)
            act.wait_ge(s_vs, B // 2)
            act.wait_ge(s_const, N_CONST_ATT)
            take_queries(0)
            attend(0, before=False, first=True)
            attend(1, second=True)
            with act.Fori(2, B - 1) as i:
                attend(i)
            attend(B - 1, more=False)
            attend(B, now=False, more=False)

            nc.scalar.preload_act_table(ACT.Sqrt)
            act.wait_ge(s_stats, 2)
            nc.scalar.activation(std[:, :], std[:, :], ACT.Sqrt).then_inc(s_std, 1)
            for n in range(2):
                act.wait_ge(s_x2t, n + 1)
                for k in range(KC):
                    nc.scalar.activation(x2T[:, k, n * HALF:(n + 1) * HALF], bank[2 * n + k][:, 0:HALF],
                                         ACT.Copy).then_inc(s_x2ts, 1)
            act.wait_ge(s_gexp, 1)
            nc.scalar.activation(pg[:, :, :], pg[:, :, :], ACT.Exp).then_inc(s_gexp, 1)

            def tile(e, b, skip_first, up=True, before=True):
                if up:
                    act.wait_ge(s_h, B * e + b + 1)
                    if not (skip_first and b < 2):
                        act.wait_ge(s_ug, B * e + b - 1)
                    nc.scalar.activation(th[:, b % 2, :], h_ps[b % 2][0:S, 0:F], ACT.Tanh, scale=0.5)\
                        .then_inc(s_th, 1)

            def take_g(e, b, skip_first):
                act.wait_ge(s_gt, B * e + b + 1)
                if not (skip_first and b < 2):
                    act.wait_ge(s_ye, B * e + b - 1)
                nc.scalar.activation(gT_hi[:, b % 2, :, :], gT_ps[b % 2], ACT.Copy).then_inc(s_gth, 1)

            def expert(e, first):
                for b in range(B):
                    tile(e, b, first)
                    if not first or b >= 1:
                        take_g(*((e, b - 1) if b >= 1 else (e - 1, B - 1)), first)

            expert(0, True)
            with act.Fori(1, E) as e:
                expert(e, False)
            take_g(E - 1, B - 1, False)

        @block.vector
        def _(dve):
            def norm(src, dst, times):
                for b in range(B):
                    if times == 0:
                        if b % (B // 2) == 0:
                            dve.wait_ge(s_x[b // (B // 2)], 16)
                        nc.vector.bn_stats(stats[:, b, :], src[:, b, :]).then_inc(s_st, 1)
                for b in range(B):
                    dve.wait_ge(s_st, B * times + b + 1)
                    nc.vector.bn_aggr(meanvar[:, b, :], stats[:, b, :]).then_inc(s_st2, 1)
                dve.wait_ge(s_st2, B * (times + 1))
                nc.vector.tensor_scalar(std[:, :], meanvar[:, :, 1], EPS, None, ALU.add).then_inc(s_stats, 1)
                dve.wait_ge(s_std, times + 1)
                nc.vector.reciprocal(rstd[:, :], std[:, :]).then_inc(s_rstd, 1)
                dve.wait_ge(s_rstd, times + 1)
                for b in range(B):
                    nc.vector.tensor_scalar(dst[:, b, :], src[:, b, :], meanvar[:, b, 0:1], rstd[:, b:b + 1],
                                            ALU.subtract, ALU.mult).then_inc(s_xh, 1)

            norm(x_sb, xhat, 0)
            dve.wait_ge(s_small, 48)
            for p in range(B // 2):
                dve.wait_ge(s_v, p + 1)
                nc.vector.tensor_tensor(v_sb[:, 2 * p:2 * p + 2, :], grid(bank[6 + p % 2], S, 2, D),
                                        bvo_sb[:, 0:1, :].to_broadcast([S, 2, D]), ALU.add).then_inc(s_vs, 1)

            def mask_scores(g):
                for h in range(G):
                    ins = nc.vector.tensor_tensor_reduce(
                        out=sc_sb[:, g % 2, h, :], in0=sc_ps[g % 2][:, h, :], in1=mask[:, :], scale=1.0,
                        scalar=LEAST, op0=ALU.add, op1=ALU.max, accum_out=rowmax[:, g % 2, h:h + 1])
                ins.then_inc(s_mk, 1)

            def sum_probs(b, g):
                dve.wait_ge(s_ex, NG * b + g + 1)
                nc.vector.tensor_reduce(sums[:, G * g:G * g + G], probs[:, g, :, :], AX.X, ALU.add)\
                    .then_inc(s_sum, 1)

            def recip_sums(b, first):
                dve.wait_ge(s_sum, NG * (b + 1))
                nc.vector.reciprocal(rsum[:, :], sums[:, :]).then_inc(s_rs, 1)
                dve.wait_ge(s_rs, b + 1)
                if not first:
                    dve.wait_ge(s_rt, b)
                nc.vector.tensor_copy(rexp[:, :, :], rsum[:, :].unsqueeze(2).to_broadcast([S, HEADS, HD]))\
                    .then_inc(s_re, 1)

            def norm_outputs(b, first):
                dve.wait_ge(s_rts, b + 1)
                dve.wait_ge(s_pv, NG * (b + 1))
                if not first:
                    dve.wait_ge(s_y, b)
                nc.vector.tensor_tensor(oT_sb[:, :, :], oT_ps, rT_sb[:, :, :], ALU.mult).then_inc(s_on, 1)

            def residual(b):
                at = bass.ds(b, 1)
                dve.wait_ge(s_y, b + 1)
                nc.vector.tensor_tensor(y_sb[:, :], y_ps, bvo_sb[:, 1, :], ALU.add).then_inc(s_yb, 1)
                dve.wait_ge(s_yb, b + 1)
                xb = x_sb[:, at, :].rearrange("p o d -> p (o d)")
                nc.vector.scalar_tensor_tensor(out=xb, in0=y_sb[:, :], scalar=tanh_gate[0:S, 0:1], in1=xb,
                                               op0=ALU.mult, op1=ALU.add).then_inc(s_x2, 1)
                dve.wait_ge(s_x2, b + 1)
                nc.vector.bn_stats(stats[:, at, :].rearrange("p o d -> p (o d)"), xb).then_inc(s_st, 1)

            def attend(i, now=True, before=True, last=True, first=False, second=False):
                for g in range(NG):
                    if now:
                        dve.wait_ge(s_sc, NG * i + g + 1)
                    if now and g >= 2:
                        sum_probs(i, g - 2)
                    elif before and g < 2:
                        sum_probs(i - 1, g + 2)
                    if now:
                        mask_scores(g)
                    if g == 1 and before:
                        recip_sums(i - 1, second)
                    if g == 2 and last:
                        residual(i - 2)
                if before:
                    norm_outputs(i - 1, second)

            dve.wait_ge(s_tg, 1)
            dve.wait_ge(s_const, 4)
            attend(0, before=False, last=False, first=True)
            attend(1, last=False, second=True)
            with dve.Fori(2, B) as i:
                attend(i)
            attend(B, now=False)
            residual(B - 1)

            norm(x_sb, x2n, 1)
            dve.wait_ge(s_b, 16)
            nc.vector.tensor_copy(b_rows_hi[:, :], b_rows[:, :]).then_inc(s_brow, 1)
            dve.wait_ge(s_brow, 1)
            nc.vector.tensor_tensor(b_rows_lo[:, :], b_rows[:, :], b_rows_hi[:, :], ALU.subtract).then_inc(s_brow, 1)
            for n in range(2):
                for k in range(KC):
                    at = slice(n * HALF, (n + 1) * HALF)
                    dve.wait_ge(s_x2ts, 2 * n + k + 1)
                    nc.vector.tensor_copy(x2T_hi[:, k, at], x2T[:, k, at]).then_inc(s_x2hi, 1)
                    dve.wait_ge(s_x2hi, 2 * n + k + 1)
                    nc.vector.tensor_tensor(x2T_lo[:, k, at], x2T[:, k, at], x2T_hi[:, k, at], ALU.subtract)\
                        .then_inc(s_x2lo, 1)

            steps = [0]

            def step(ins):
                steps[0] += 1
                ins.then_inc(s_chain, 1)
                dve.wait_ge(s_chain, steps[0])

            def over_e(t):
                return t.unsqueeze(2).to_broadcast([S, B, ER])

            dve.wait_ge(s_const, N_CONST)
            dve.wait_ge(s_gl, 32)
            dve.wait_ge(s_lg, 1)
            step(nc.vector.tensor_tensor(pg[:, :, :], lg_ps, gb_sb[:, :].unsqueeze(1).to_broadcast([S, B, ER]), ALU.add))
            step(nc.vector.tensor_reduce(gsum[:, :], pg[:, :, :], AX.X, ALU.max))
            nc.vector.tensor_tensor(pg[:, :, :], pg[:, :, :], over_e(gsum[:, :]), ALU.subtract).then_inc(s_gexp, 1)
            dve.wait_ge(s_gexp, 2)
            step(nc.vector.tensor_reduce(gsum[:, :], pg[:, :, :], AX.X, ALU.add))
            step(nc.vector.reciprocal(first[:, :], gsum[:, :]))
            step(nc.vector.tensor_tensor(pg[:, :, :], pg[:, :, :], over_e(first[:, :]), ALU.mult))
            for n in range(2):
                p = pg if n == 0 else pg2
                step(nc.vector.tensor_reduce(top[:, n, :], p[:, :, :], AX.X, ALU.max))
                step(nc.vector.tensor_tensor(eq[:, :, :], p[:, :, :], over_e(top[:, n, :]), ALU.is_equal))
                step(nc.vector.scalar_tensor_tensor(out=eq[:, :, :], in0=eq[:, :, :], scalar=-float(ER),
                                                    in1=iota8[:, :, :], op0=ALU.mult, op1=ALU.add))
                step(nc.vector.tensor_reduce(first[:, :], eq[:, :, :], AX.X, ALU.min))
                step(nc.vector.tensor_tensor(hot[:, n, :, :], eq[:, :, :], over_e(first[:, :]), ALU.is_equal))
                if n == 0:
                    step(nc.vector.scalar_tensor_tensor(out=pg2[:, :, :], in0=hot[:, 0, :, :], scalar=-4.0,
                                                        in1=pg[:, :, :], op0=ALU.mult, op1=ALU.add))
            step(nc.vector.tensor_tensor(eq[:, :, :], hot[:, 0, :, :], over_e(top[:, 0, :]), ALU.mult))
            step(nc.vector.tensor_tensor(pg2[:, :, :], hot[:, 1, :, :], over_e(top[:, 1, :]), ALU.mult))
            step(nc.vector.tensor_tensor(cw[:, :, 0:ER], eq[:, :, :], pg2[:, :, :], ALU.add))

            def gate(e, b, first):
                h = h_ps[b % 2]
                dve.wait_ge(s_th, B * e + b + 1)
                nc.vector.scalar_tensor_tensor(out=ug[:, b % 2, :], in0=th[:, b % 2, :], scalar=1.0,
                                               in1=h[0:S, 0:F], op0=ALU.add, op1=ALU.mult).then_inc(s_ug, 1)
                dve.wait_ge(s_ug, B * e + b + 1)
                if not (first and b < 2):
                    dve.wait_ge(s_gt, B * e + b - 1)
                nc.vector.scalar_tensor_tensor(out=gg[:, b % 2, :], in0=ug[:, b % 2, :], scalar=0.5,
                                               in1=h[0:S, F:2 * F], op0=ALU.mult, op1=ALU.mult).then_inc(s_gg, 1)

            def take_low(e, b):
                dve.wait_ge(s_gth, B * e + b + 1)
                nc.vector.tensor_tensor(gT_lo[:, b % 2, :, :], gT_ps[b % 2], gT_hi[:, b % 2, :, :], ALU.subtract)\
                    .then_inc(s_gtl, 1)

            def collect(e, b):
                dve.wait_ge(s_ye, B * e + b + 1)
                nc.vector.scalar_tensor_tensor(out=acc[:, b, :], in0=ye_ps[b % 2][0:S, 0:D],
                                               scalar=cw[:, b, bass.ds(e, 1)], in1=acc[:, b, :],
                                               op0=ALU.mult, op1=ALU.add).then_inc(s_acc, 1)

            def expert(e, first):
                for b in range(B):
                    gate(e, b, first)
                    if not first or b >= 1:
                        take_low(*((e, b - 1) if b >= 1 else (e - 1, B - 1)))
                    if not first or b >= 2:
                        collect(*((e, b - 2) if b >= 2 else (e - 1, B - 2 + b)))

            expert(0, True)
            with dve.Fori(1, E) as e:
                expert(e, False)
            take_low(E - 1, B - 1)
            collect(E - 1, B - 2)
            collect(E - 1, B - 1)
            dve.wait_ge(s_acc, B * E)
            for b in range(B):
                nc.vector.scalar_tensor_tensor(out=x2n[:, b, :], in0=acc[:, b, :], scalar=tanh_gate[0:S, 1:2],
                                               in1=x_sb[:, b, :], op0=ALU.mult, op1=ALU.add).then_inc(s_fin, 1)


def kernel(**inputs):
    import numpy as np
    import concourse.bacc as bacc
    from concourse.bass_utils import run_bass_kernel_spmd

    def rows(a):
        return np.ascontiguousarray(a.reshape(KC, 128, -1).transpose(1, 0, 2))

    a = {k: np.asarray(v) for k, v in inputs.items()}
    w1 = np.concatenate([a["L0_ffn_rw1"], a["L0_ffn_sw1"]])
    w2 = np.concatenate([a["L0_ffn_rw2"], a["L0_ffn_sw2"]])
    w1 = w1.reshape(E, KC, 128, 2 * F)
    w2 = w2.reshape(E, 1, KC, 128, D).transpose(0, 1, 3, 2, 4).reshape(E, 1, 128, KC * D)
    ctx = a["ctx_1024"][:, :S, :].transpose(2, 0, 1).reshape(D, TOK)
    arrays = {
        "x": np.ascontiguousarray(a["x"].transpose(1, 0, 2)),
        "ctxT": rows(ctx),
        "wqT": rows(a["L0_xattn_Wq"].T), "wkT": rows(a["L0_xattn_Wk"].T),
        "wvT": rows(a["L0_xattn_Wv"].T), "woT": rows(a["L0_xattn_Wo"].T),
        "bqk": np.ascontiguousarray(np.stack([a["L0_xattn_bq"], a["L0_xattn_bk"]]).reshape(2, KC, 128).transpose(2, 0, 1)),
        "bvo": np.stack([a["L0_xattn_bv"], a["L0_xattn_bo"]]),
        "gates": np.concatenate([a["g_xattn"], a["g_ffn"]]),
        "gate_w": rows(a["L0_ffn_gate_w"]),
        "gate_b": a["L0_ffn_gate_b"],
        "w_all": np.ascontiguousarray(np.concatenate([w1, w2], axis=1).reshape(E * PIECES, 128, PW)),
        "b_all": np.concatenate([a["L0_ffn_rb1"].ravel(), a["L0_ffn_sb1"].ravel(),
                                 a["L0_ffn_rb2"].ravel(), a["L0_ffn_sb2"].ravel()]).reshape(-1, 128),
    }
    nc = bacc.Bacc("TRN2", target_bir_lowering=False, num_devices=1)
    aps = [nc.dram_tensor(f"in_{n}", v.shape, F32, kind="ExternalInput").ap() for n, v in arrays.items()]
    out = nc.dram_tensor("out", (B, S, D), F32, kind="ExternalOutput").ap()
    block_kernel(nc, *aps, out)
    r = run_bass_kernel_spmd(nc, [{f"in_{n}": v for n, v in arrays.items()}], core_ids=[0])
    return r.results[0]["out"]
```

```python
from contextlib import ExitStack

import concourse.bass as bass
from concourse import mybir

BF16 = mybir.dt.bfloat16
I32 = mybir.dt.int32
U32 = mybir.dt.uint32
F32 = mybir.dt.float32
F32R = mybir.dt.float32r
ALU = mybir.AluOpType
ACT = mybir.ActivationFunctionType
AX = mybir.AxisListType

B, S, D = 8, 112, 256
HEADS, HD = 16, 16
KC = D // 128
TOK = B * S
HALF = TOK // 2
G = 4
NG = HEADS // G
E = 9
ER = 8
F = 256
PIECES = 3
PW = 512
EPS = 1e-5
NEG = -1e30
LEAST = -3e38
PART = 128
TOP = 2
NT = TOP * TOK // PART + ER - 1
XG = 4
NV = 4


def block_kernel(nc, x, ctxT, wqT, wkT, wvT, woT, bqk, bvo, gates, gate_w, gate_b, w_all, b_routed,
                 b1_shared, b2_shared, out):
    with ExitStack() as ctx:
        def sb(name, shape, dt=F32, scope=ctx):
            return scope.enter_context(nc.sbuf_tensor(name, shape, dt))

        def sem(name):
            return ctx.enter_context(nc.semaphore(name))

        x_sb = sb("x_sb", [S, B, D])
        w_hi = sb("w_hi", [128, E * PIECES * PW], F32R)
        w_lo = sb("w_lo", [128, E * PIECES * PW], F32R)
        ident = sb("ident", [128, 128])
        gate_cols = sb("gate_cols", [128, 2])
        tanh_gate = sb("tanh_gate", [128, 2])
        stats = sb("stats", [S, B, 6])
        meanvar = sb("meanvar", [S, B, 2])
        std = sb("std", [S, B])
        rstd = sb("rstd", [S, B])

        att = ctx.enter_context(ExitStack())
        wv_sb = sb("wv_sb", [128, KC, D], scope=att)
        wo_sb = sb("wo_sb", [128, KC, D], scope=att)
        bqk_sb = sb("bqk_sb", [128, 2, KC], scope=att)
        bvo_sb = sb("bvo_sb", [S, 2, D], scope=att)
        qT = sb("qT", [128, KC, TOK], scope=att)
        kT = sb("kT", [128, KC, TOK], scope=att)
        xhat = sb("xhat", [S, B, D], scope=att)
        v_sb = xhat
        mask = sb("mask", [S, S], scope=att)
        q_now = sb("q_now", [128, KC, S], scope=att)
        k_diag = sb("k_diag", [128, NG, G, 4, S], scope=att)
        v_pad = sb("v_pad", [S, HEADS // 2, 2, 2, HD], scope=att)
        raw = sb("raw", [128, PIECES, PW], scope=att)
        sc_sb = sb("sc_sb", [S, 2, G, S], scope=att)
        rowmax = sb("rowmax", [S, 2, G], scope=att)
        sums = sb("sums", [S, HEADS], scope=att)
        rsum = sb("rsum", [S, HEADS], scope=att)
        probs = sb("probs", [S, NG, G, S], scope=att)
        early = att.enter_context(ExitStack())
        wq_sb = sb("wq_sb", [128, KC, D], scope=early)
        wk_sb = sb("wk_sb", [128, KC, D], scope=early)
        ctxT_sb = sb("ctxT_sb", [128, KC, TOK], scope=early)
        xhatT = sb("xhatT", [128, KC, HALF], scope=early)
        early.close()
        pT_sb = sb("pT_sb", [S, 2, G, S], scope=att)
        rexp = sb("rexp", [S, HEADS, HD], scope=att)
        rT_sb = sb("rT_sb", [128, KC, S], scope=att)
        oT_sb = sb("oT_sb", [128, KC, S], scope=att)
        y_sb = sb("y_sb", [S, D], scope=att)
        att.close()

        x2n_all = sb("x2n", [128, B * D])
        x2n = x2n_all[0:S, :].rearrange("p (b d) -> p b d", b=B)
        gw_sb = sb("gw_sb", [128, KC, ER])
        gb_sb = sb("gb_sb", [S, ER])
        b1s = sb("b1s", [128, 2 * KC])
        b1s_half = sb("b1s_half", [128, KC])
        b2s = sb("b2s", [S, D])
        bias = sb("bias", [128, 2 * F + D], F32R)
        pg = sb("pg", [S, B, ER])
        pg2 = sb("pg2", [S, B, ER])
        top = sb("top", [S, TOP, B])
        gsum = sb("gsum", [S, B])
        eq = sb("eq", [S, B, ER])
        first = sb("first", [S, B])
        hot = sb("hot", [S, TOP, B, ER])
        both = sb("both", [S, 2 * B, ER], BF16)
        iota8 = sb("iota8", [S, B, ER])
        before = sb("before", [S, S], BF16)
        ones_b = sb("ones_b", [S, 128], BF16)
        iota_j = sb("iota_j", [128, ER, 7])
        less = sb("less", [128, ER, ER])
        iota_t = sb("iota_t", [128, NT, ER])
        iota_tok = sb("iota_tok", [S, NT])
        iota_p = sb("iota_p", [S, PART])
        row8 = sb("row8", [128, 1])
        dump = sb("dump", [128, NT])
        cnt_gt = sb("cnt_gt", [128, ER, 7])
        tiles = sb("tiles", [128, ER])
        t_less = sb("t_less", [128, ER, ER])
        tile0 = sb("tile0", [128, ER])
        tile_e = sb("tile_e", [128, NT])
        tile_ei = sb("tile_ei", [1, NT + XG], I32)
        e_hot = sb("e_hot", [128, NT + 1], F32R)
        slots = sb("slots", [S, B, ER])
        slot = sb("slot", [S, TOP * B])
        slot_ti = sb("slot_ti", [S, TOP * B], I32)
        slot_t = sb("slot_t", [S, TOP * B])
        slot_p = sb("slot_p", [S, TOP * B])
        vals = sb("vals", [S, TOP * B, NV])
        top_hi = sb("top_hi", [S, TOP * B], F32R)
        slot_w = sb("slot_w", [128, NT + 1])
        late = sb("late", [128, NT])
        empty = sb("empty", [128, NT])
        smap = sb("smap", [128, NV, NT])
        tok_i = sb("tok_i", [128, NT + 1], U32)
        row_i = sb("row_i", [128, NT + 1], U32)
        eq_t = sb("eq_t", [S, TOP * B, NT])
        t_ge = sb("t_ge", [128, NT, ER])
        sel_up = sb("sel_up", [128, 2, 1], F32R)
        sel_down = sb("sel_down", [128, 2, 1], F32R)
        gT_hi = sb("gT_hi", [128, 2, 2, 128], F32R)
        gT_lo = sb("gT_lo", [128, 2, 2, 128], F32R)
        ye = sb("ye", [128, 2, D])
        split_b = ctx.enter_context(ExitStack())
        b_raw = sb("b_raw", [ER, 2 * F + D], scope=split_b)
        b_hi = sb("b_hi", [ER, 2 * F + D], F32R, scope=split_b)
        b_lo = sb("b_lo", [ER, 2 * F + D], F32R, scope=split_b)
        slot_e = sb("slot_e", [S, TOP, B, ER], scope=split_b)
        split_b.close()
        xT_hi = sb("xT_hi", [128, 2, KC, 128], F32R)
        xT_lo = sb("xT_lo", [128, 2, KC, 128], F32R)
        th = sb("th", [128, 2, F])
        ug = sb("ug", [128, 2, F])
        gg = sb("gg", [128, 2, F])
        x_flat = x_sb[:, :, :].rearrange("p b d -> p (b d)")
        acc = x2n

        route = ctx.enter_context(ExitStack())
        x2T_hi = sb("x2T_hi", [128, KC, TOK], F32R, scope=route)
        x2T = sb("x2T", [128, KC, TOK], scope=route)
        x2T_lo = sb("x2T_lo", [128, KC, TOK], F32R, scope=route)
        g_sh = x2T
        gs_hi = sb("gs_hi", [128, KC, TOK], F32R, scope=route)
        gs_lo = sb("gs_lo", [128, KC, TOK], F32R, scope=route)
        abu = sb("abu", [128, 3 * HALF], scope=route)
        a_sh = [abu[:, 0:HALF], x2n_all[:, 0:HALF]]
        b_sh = [abu[:, HALF:2 * HALF], x2n_all[:, HALF:2 * HALF]]
        u_sh = [abu[:, 2 * HALF:3 * HALF], x2n_all[:, 2 * HALF:3 * HALF]]
        slot_hot = sb("slot_hot", [S, TOP * B, PART], F32R, scope=route)
        tile_val = sb("tile_val", [S, TOP * B, NV, NT], F32R, scope=route)
        route.close()
        xg = sb("xg", [128, XG, D])
        y_back = sb("y_back", [S, TOP, B, D])
        x_rows = nc.dram_tensor("x_rows", [TOK, D], F32, kind="Internal").ap()
        y_rows = nc.dram_tensor("y_rows", [TOP * TOK + NT * PART, D], F32, kind="Internal").ap()

        bank = [ctx.enter_context(nc.psum_tensor(f"bank{n}", [128, 512], F32)) for n in range(8)]

        def grid(t, p, n, w):
            return t[0:p, 0:n * w].rearrange("p (n w) -> p n w", n=n)

        sc_ps = [grid(bank[n], S, G, S) for n in (0, 1)]
        pT_ps = [grid(bank[n], S, G, S) for n in (2, 3)]
        oT_ps = grid(bank[4], 128, KC, S)
        rT_ps = grid(bank[5], 128, KC, S)
        y_ps = bank[6][0:S, 0:D]
        h_ps = [bank[n] for n in (0, 1)]
        xt_ps = [grid(bank[n], 128, KC, 128) for n in (2, 3)]
        gt_ps = [grid(bank[n], 128, 2, 128) for n in (6, 7)]
        ye_ps = [bank[n] for n in (4, 5)]
        lg_ps = grid(bank[6], S, B, ER)
        pos_ps = grid(bank[4], S, B, ER)
        cnt_ps = bank[5][:, 0:ER]
        map_ps = grid(bank[7], 128, NV, NT)

        s_wk, s_wv, s_wq, s_small, s_b, s_wo = (
            sem(n) for n in ("wk_in", "wv_in", "wq_in", "small_in", "biases_in", "wo_in"))
        s_x = [sem(f"x_in{n}") for n in range(2)]
        s_ctx = [sem(f"ctx_in{n}") for n in range(2)]
        s_raw = [sem(f"raw_in{j}") for j in range(PIECES)]
        s_const, s_zero = sem("consts_ready"), sem("zeros_ready")
        s_k, s_kt = sem("k_projected"), sem("kT_ready")
        s_v, s_vs = sem("v_projected"), sem("v_ready")
        s_st2 = sem("meanvars_ready")
        s_st, s_stats, s_std, s_rstd, s_xh = (
            sem("stats_ready"), sem("meanvar_ready"), sem("std_ready"), sem("rstd_ready"), sem("xhat_ready"))
        s_xt, s_xts = sem("xhat_transposed"), sem("xhatT_ready")
        s_q, s_qt = sem("q_projected"), sem("qT_ready")
        s_tg = sem("tanh_gate_ready")
        s_qn = [sem(f"q_now{k}_ready") for k in range(KC)]
        s_vp = sem("v_pad_ready")
        s_kd = [sem(f"k_diag_in{g}") for g in range(NG // 2)]
        s_sc, s_mk, s_sh, s_ex, s_sum = (
            sem("scores_ready"), sem("scores_masked"), sem("scores_shifted"),
            sem("probs_ready"), sem("sums_ready"))
        s_pt, s_pts, s_pv = sem("probs_transposed"), sem("pT_ready"), sem("pv_done")
        s_rs, s_re, s_rt, s_rts = (
            sem("rsum_ready"), sem("rexp_ready"), sem("rsum_transposed"), sem("rT_ready"))
        s_on, s_y, s_yb, s_x2 = sem("oT_ready"), sem("y_projected"), sem("y_biased"), sem("x2_ready")
        s_whi, s_wlo = sem("w_hi_ready"), sem("w_lo_ready")
        s_brow, s_bias = sem("bias_rows_split"), sem("bias_in")
        s_fc = sem("expert_consts_ready")
        s_x2hi, s_x2t32 = sem("x2T_hi_ready"), sem("x2T_ready")
        s_xr, s_hot, s_pos, s_cnt = sem("x_rows_stored"), sem("hot_ready"), sem("pos_ready"), sem("counts_ready")
        s_te, s_eh = sem("tile_experts_ready"), sem("e_hot_ready")
        s_tv, s_map, s_idx = sem("tile_val_ready"), sem("map_ready"), sem("slot_rows_ready")
        s_us, s_tha, s_aa, s_bb, s_pu = (
            sem("shared_up"), sem("shared_tanh"), sem("shared_a"), sem("shared_b"), sem("shared_u"))
        s_gs, s_gsh, s_gsl, s_ys, s_yse = (
            sem("shared_g"), sem("shared_g_hi"), sem("shared_g_lo"), sem("shared_y"), sem("shared_y_out"))
        s_xg = [sem(f"x_gathered{n}") for n in range(XG)]
        s_yw = [sem(f"y_scattered{n}") for n in range(2)]
        s_xtp, s_xth, s_xtl = (
            sem("xg_transposed"), sem("xT_hi_ready"), sem("xT_lo_ready"))
        s_xs, s_rsum = sem("shared_added"), sem("routed_summed")
        s_yback = [sem(f"y_back_in{b}") for b in range(B)]
        s_gl = sem("gate_in")
        s_chain = sem("router_step")
        s_x2t, s_x2lo = sem("x2n_transposed"), sem("x2T_lo_ready")
        s_lg = sem("logits_ready")
        s_gexp = sem("gate_exp_ready")
        s_h, s_th, s_ug, s_gg, s_gt, s_gth, s_gtl, s_ye, s_yo = (
            sem("h_ready"), sem("tanh_ready"), sem("u_ready"), sem("g_ready"), sem("g_transposed"),
            sem("gT_hi_ready"), sem("gT_lo_ready"), sem("ye_ready"), sem("ye_weighted"))
        s_fin, s_out = sem("out_ready"), sem("out_stored")

        block = ctx.enter_context(nc.Block())

        def head_rows(h):
            return slice(HD * (h % 8), HD * (h % 8) + HD)

        @block.sync
        def _(sp):
            for n in range(2):
                sp.dma_start(x_sb[:, n * B // 2:(n + 1) * B // 2, :], x[:, n * B // 2:(n + 1) * B // 2, :])\
                    .then_inc(s_x[n], 16)
            sp.dma_start(bqk_sb[:, :, :], bqk).then_inc(s_small, 16)
            sp.dma_start(bvo_sb[:, :, :], bvo.partition_broadcast(S)).then_inc(s_small, 16)
            sp.dma_start(gate_cols[:, :], gates.partition_broadcast(128)).then_inc(s_small, 16)
            sp.dma_start(wv_sb[:, :, :], wvT).then_inc(s_wv, 16)
            sp.dma_start(wq_sb[:, :, :], wqT).then_inc(s_wq, 16)
            sp.dma_start(wo_sb[:, :, :], woT).then_inc(s_wo, 16)
            for j in range(PIECES):
                sp.dma_start(raw[:, j, :], w_all[j]).then_inc(s_raw[j], 16)

            def load_keys(p, h):
                g = h // G
                sp.dma_start(k_diag[head_rows(h), g::2, h % G, bass.ds(p % 2 * 2, 2), :],
                             kT[head_rows(h), :, bass.ds(p * (2 * S), 2 * S)]).then_inc(s_kd[g], 16)

            def load_weights(e, j):
                sp.wait_ge(s_wlo, PIECES * (e - 1) + j + 1)
                sp.dma_start(raw[:, j, :], w_all[bass.ds(PIECES * e + j, 1)].rearrange("a p n -> (a p) n"))\
                    .then_inc(s_raw[j], 16)

            def load_ahead(p, first=False, more=True):
                for b in range(2):
                    for g in range(NG):
                        if g:
                            load_weights(2 * p + 1 + b, g - 1)
                        if more and b == 0:
                            for h in (2 * g, 2 * g + 1):
                                if h % G == 0:
                                    if not first:
                                        sp.wait_ge(s_sc, NG * (2 * p - 1) + h // G + 3)
                                    sp.wait_ge(s_kd[h // G], 16 * G * (p + 1))
                                load_keys(p + 1, h)

            sp.wait_ge(s_zero, 1)
            sp.wait_ge(s_kt, KC)
            for h in range(HEADS // 2):
                load_keys(0, h)
            load_ahead(0, first=True)
            sp.wait_ge(s_kt, 2 * KC)
            with sp.Fori(1, B // 2 - 1) as p:
                load_ahead(p)
            load_ahead(B // 2 - 1, more=False)
            sp.wait_ge(s_x2, B)
            sp.wait_ge(s_wlo, PIECES * E)
            sp.dma_start(gw_sb[:, :, :], gate_w).then_inc(s_gl, 16)
            sp.dma_start(gb_sb[:, :], gate_b.partition_broadcast(S)).then_inc(s_gl, 16)
            sp.dma_start(b_raw[:, :], b_routed).then_inc(s_b, 16)
            sp.dma_start(b1s[:, :], b1_shared).then_inc(s_b, 16)
            sp.dma_start(b2s[:, :], b2_shared.partition_broadcast(S)).then_inc(s_b, 16)
            for n in range(2):
                half = slice(n * B // 2, (n + 1) * B // 2)
                sp.wait_ge(s_xh, B + (n + 1) * B // 2)
                sp.dma_start(x_rows.rearrange("(b s) d -> s b d", s=S)[:, half, :], x2n[:, half, :])\
                    .then_inc(s_xr, 16)
            sp.wait_ge(s_brow, 2)
            sp.wait_ge(s_fc, 1)
            sp.dma_start(bias[0:ER, :].bitcast(F32), b_hi[:, :].bitcast(F32)).then_inc(s_bias, 16)
            sp.dma_start(bias[ER:2 * ER, :].bitcast(F32), b_lo[:, :].bitcast(F32)).then_inc(s_bias, 16)
            for n in range(2):
                sp.wait_ge(s_yw[n], 16 * ((NT + 1 - n) // 2))
            for b in range(B):
                sp.dma_start(y_back[:, :, b, :],
                             y_rows[0:TOP * TOK, :].rearrange("(k b s) d -> s k b d", k=TOP, s=S)[:, :, b, :])\
                    .then_inc(s_yback[b], 16)
            for b in range(B):
                sp.wait_ge(s_fin, b + 1)
                sp.dma_start(out[b], acc[:, b, :]).then_inc(s_out, 16)
            sp.wait_ge(s_out, 16 * B)

        @block.gpsimd
        def _(pool):
            nc.gpsimd.memset(ident[:, :], 0.0).then_inc(s_const, 1)
            nc.gpsimd.memset(mask[:, :], 0.0).then_inc(s_const, 1)
            pool.wait_ge(s_const, 2)
            nc.gpsimd.affine_select(out=ident[:, :], in_=ident[:, :], compare_op=ALU.not_equal, fill=1.0,
                                    base=0, pattern=[[-1, 128]], channel_multiplier=1).then_inc(s_const, 1)
            nc.gpsimd.affine_select(out=mask[:, :], in_=mask[:, :], compare_op=ALU.is_ge, fill=NEG,
                                    base=0, pattern=[[-1, S]], channel_multiplier=1).then_inc(s_const, 1)
            nc.gpsimd.memset(k_diag[:, :, :, :, :], 0.0).then_inc(s_zero, 1)
            nc.gpsimd.memset(v_pad[:, :, :, :, :], 0.0).then_inc(s_const, 1)

            def split(e, j):
                    at = bass.ds(PW * (PIECES * e + j), PW)
                    pool.wait_ge(s_whi, PIECES * e + j + 1)
                    nc.gpsimd.tensor_tensor(w_lo[:, at], raw[:, j, :], w_hi[:, at], ALU.subtract)\
                        .then_inc(s_wlo, 1)

            def shift(b, g):
                pool.wait_ge(s_mk, NG * b + g + 1)
                nc.gpsimd.tensor_tensor(sc_sb[:, g % 2, :, :], sc_sb[:, g % 2, :, :],
                                        rowmax[:, g % 2, :].unsqueeze(2).to_broadcast([S, G, S]), ALU.subtract)\
                    .then_inc(s_sh, 1)

            with pool.Fori(0, B) as b:
                for g in range(NG):
                    shift(b, g)
                    if g:
                        split(b, g - 1)
            for j in range(PIECES):
                split(E - 1, j)
            pool.wait_ge(s_wlo, PIECES * E)
            pool.wait_ge(s_x2, B)
            nc.gpsimd.memset(bias[:, :].bitcast(F32), 0.0).then_inc(s_fc, 1)
            small = dict(allow_small_or_imprecise_dtypes=True)
            nc.gpsimd.iota(iota8[:, :, :], pattern=[[0, B], [1, ER]], base=0, channel_multiplier=0, **small)
            nc.gpsimd.iota(iota_j[:, :, :], pattern=[[0, ER], [PART, 7]], base=0, channel_multiplier=0, **small)
            nc.gpsimd.iota(iota_t[:, :, :], pattern=[[1, NT], [0, ER]], base=0, channel_multiplier=0, **small)
            nc.gpsimd.iota(iota_tok[:, :], pattern=[[1, NT]], base=0, channel_multiplier=0, **small)
            nc.gpsimd.iota(iota_p[:, :], pattern=[[1, PART]], base=0, channel_multiplier=0, **small)
            nc.gpsimd.iota(row8[:, :], pattern=[[0, 1]], base=0, channel_multiplier=1, **small).then_inc(s_fc, 1)
            nc.gpsimd.iota(dump[:, :], pattern=[[-PART, NT]], base=-TOP * TOK, channel_multiplier=-1, **small)
            nc.gpsimd.iota(vals[:, :, 1], pattern=[[S, TOP * B]], base=0, channel_multiplier=1, **small)
            nc.gpsimd.memset(vals[:, :, 0], 1.0)
            nc.gpsimd.memset(ones_b[:, :], 1.0)
            nc.gpsimd.memset(both[:, 0:B, :], 0.0)
            nc.gpsimd.memset(before[:, :], 1.0)
            nc.gpsimd.memset(less[:, :, :], 1.0).then_inc(s_fc, 1)
            pool.wait_ge(s_fc, 3)
            nc.gpsimd.affine_select(out=before[:, :], in_=before[:, :], compare_op=ALU.is_gt, fill=0.0,
                                    base=0, pattern=[[1, S]], channel_multiplier=-1)
            nc.gpsimd.affine_select(out=less[:, :, :], in_=less[:, :, :], compare_op=ALU.is_gt, fill=0.0,
                                    base=0, pattern=[[1, ER], [-1, ER]], channel_multiplier=0).then_inc(s_fc, 1)

            for n in range(2):
                for k in range(KC):
                    at = slice(n * HALF, (n + 1) * HALF)
                    pool.wait_ge(s_x2t32, 2 * n + k + 1)
                    pool.wait_ge(s_x2hi, 2 * n + k + 1)
                    nc.gpsimd.tensor_tensor(x2T_lo[:, k, at], x2T[:, k, at], x2T_hi[:, k, at], ALU.subtract)\
                        .then_inc(s_x2lo, 1)
            for n in range(2):
                for m in range(KC):
                    t = 2 * n + m
                    a, b, u, at = a_sh[t % 2], b_sh[t % 2], u_sh[t % 2], slice(n * HALF, (n + 1) * HALF)
                    pool.wait_ge(s_aa, t + 1)
                    nc.gpsimd.tensor_tensor(u, u, a, ALU.mult).then_inc(s_pu, 1)
                    pool.wait_ge(s_bb, t + 1)
                    pool.wait_ge(s_pu, t + 1)
                    nc.gpsimd.tensor_tensor(g_sh[:, m, at], u, b, ALU.mult).then_inc(s_gs, 1)

            def gather(t):
                if t >= XG:
                    pool.wait_ge(s_xtp, t - XG + 1)
                nc.gpsimd.indirect_dma_start(
                    xg[:, t % XG, :], None, x_rows, bass.IndirectOffsetOnAxis(ap=tok_i[:, t:t + 1], axis=0),
                    bounds_check=TOK - 1).then_inc(s_xg[t % XG], 16)

            def scatter(t):
                pool.wait_ge(s_yo, t + 1)
                nc.gpsimd.indirect_dma_start(
                    y_rows, bass.IndirectOffsetOnAxis(ap=row_i[:, t:t + 1], axis=0), ye[:, t % 2, :], None,
                    bounds_check=TOP * TOK + NT * PART - 1).then_inc(s_yw[t % 2], 16)

            pool.wait_ge(s_idx, 1)
            pool.wait_ge(s_xr, 32)
            pool.wait_ge(s_us, 8)
            for t in range(NT + XG + 1):
                if t < NT:
                    gather(t)
                if t > XG:
                    scatter(t - XG - 1)

        @block.tensor
        def _(pe):
            def project(ps, w, rhs, m, n):
                for k in range(KC):
                    last = nc.tensor.matmul(ps[:, 0:HALF], w[:, k, m * 128:(m + 1) * 128],
                                            rhs[:, k, n * HALF:(n + 1) * HALF], start=(k == 0), stop=(k == KC - 1))
                return last

            def keys(n):
                pe.wait_ge(s_ctx[n], 16)
                if n:
                    pe.wait_ge(s_xts, KC)
                for m in range(KC):
                    project(bank[2 * n + m], wk_sb, ctxT_sb, m, n).then_inc(s_k, 1)

            def turn_xhat(n):
                for b in range(4 * n, 4 * n + 4):
                    pe.wait_ge(s_xh, b + 1)
                    for k in range(KC):
                        mm = nc.tensor.transpose(bank[2 * n + 2 + k][:, (b % 4) * S:(b % 4 + 1) * S],
                                                 xhat[:, b, k * 128:(k + 1) * 128], ident[0:S, 0:S])
                mm.then_inc(s_xt, 1)

            def queries(n):
                pe.wait_ge(s_xts, KC * (n + 1))
                for m in range(KC):
                    if n:
                        pe.wait_ge(s_kt, KC + m + 1)
                    project(bank[4 - 2 * n + m], wq_sb, xhatT, m, 0).then_inc(s_q, 1)

            def values(p):
                if p >= 2:
                    pe.wait_ge(s_vs, p - 1)
                for b in (2 * p, 2 * p + 1):
                    for k in range(KC):
                        mm = nc.tensor.matmul(bank[6 + p % 2][0:S, (b % 2) * D:(b % 2 + 1) * D],
                                              ctxT_sb[:, k, b * S:(b + 1) * S], wv_sb[:, k, :],
                                              start=(k == 0), stop=(k == KC - 1))
                mm.then_inc(s_v, 1)

            pe.wait_ge(s_wk, 16)
            keys(0)
            pe.wait_ge(s_const, 3)
            turn_xhat(0)
            pe.wait_ge(s_wq, 16)
            queries(0)
            pe.wait_ge(s_wv, 16)
            values(0)

            def scores(b, g, first):
                if g % 2 == 0:
                    pe.wait_ge(s_qn[g // 2], b + 1)
                pe.wait_ge(s_kd[g % 2], 16 * G * (b // 2 + 1))
                if not (first and g < 2):
                    pe.wait_ge(s_mk, NG * b + g - 1)
                nc.tensor.matmul(sc_ps[g % 2], q_now[:, g // 2, :],
                                 k_diag[:, g, :, bass.ds(b % 4, 1), :].rearrange("p h o s -> p h (o s)"),
                                 start=True, stop=True).then_inc(s_sc, 1)

            def turn(b, g, first):
                pe.wait_ge(s_ex, NG * b + g + 1)
                if not (first and g < 2):
                    pe.wait_ge(s_pts, NG * b + g - 1)
                for h in range(G):
                    mm = nc.tensor.transpose(pT_ps[g % 2][:, h, :], probs[:, g, h, :], ident[0:S, 0:S])
                mm.then_inc(s_pt, 1)

            def pv(b, g, first):
                pe.wait_ge(s_pts, NG * b + g + 1)
                if g == 0:
                    pe.wait_ge(s_vp, b + 1)
                    if not first:
                        pe.wait_ge(s_on, b)
                for h in range(G):
                    pair = 2 * g + h // 2
                    at = 32 * (pair % 4)
                    mm = nc.tensor.matmul(oT_ps[at:at + 32, g // 2, :],
                                          v_pad[:, pair, h % 2, :, :].rearrange("p a d -> p (a d)"),
                                          pT_sb[:, g % 2, h, :], start=(h % 2 == 0), stop=(h % 2 == 1))
                mm.then_inc(s_pv, 1)

            def turn_rsum(b, first):
                pe.wait_ge(s_re, b + 1)
                if not first:
                    pe.wait_ge(s_rts, b)
                for k in range(KC):
                    mm = nc.tensor.transpose(rT_ps[:, k, :],
                                             rexp[:, 8 * k:8 * k + 8, :].rearrange("p a d -> p (a d)"),
                                             ident[0:S, 0:S])
                mm.then_inc(s_rt, 1)

            def out_proj(b, first):
                pe.wait_ge(s_on, b + 1)
                if first:
                    pe.wait_ge(s_wo, 16)
                    pe.wait_ge(s_vs, B // 2)
                else:
                    pe.wait_ge(s_yb, b)
                for k in range(KC):
                    mm = nc.tensor.matmul(y_ps, oT_sb[:, k, :], wo_sb[:, k, :], start=(k == 0), stop=(k == KC - 1))
                mm.then_inc(s_y, 1)

            def attend(i, now=True, before=True, last=True, first=False, second=False, third=False):
                for g in range(NG):
                    if now:
                        scores(i, g, first)
                    if last and g == 1:
                        out_proj(i - 2, third)
                    if before:
                        turn(i - 1, g, second)
                        if g:
                            pv(i - 1, g - 1, second)
                if before:
                    turn_rsum(i - 1, second)
                    pv(i - 1, NG - 1, second)

            pe.wait_ge(s_kt, KC)
            scores(0, 0, True)
            values(1)
            scores(0, 1, True)
            keys(1)
            scores(0, 2, True)
            pe.wait_ge(s_qt, KC)
            turn_xhat(1)
            scores(0, 3, True)
            queries(1)
            values(2)
            values(3)
            pe.wait_ge(s_qt, 2 * KC)
            attend(1, last=False, second=True)
            attend(2, third=True)
            with pe.Fori(3, B) as i:
                attend(i)
            attend(B, now=False)
            out_proj(B - 1, False)

            for n in range(2):
                for b in range(4 * n, 4 * n + 4):
                    pe.wait_ge(s_xh, B + b + 1)
                    for k in range(KC):
                        mm = nc.tensor.transpose(bank[2 * n + k][:, (b % 4) * S:(b % 4 + 1) * S],
                                                 x2n[:, b, k * 128:(k + 1) * 128], ident[0:S, 0:S])
                mm.then_inc(s_x2t, 1)
            pe.wait_ge(s_gl, 32)
            for b in range(B):
                pe.wait_ge(s_x2t32, KC * (b // 4 + 1))
                for k in range(KC):
                    mm = nc.tensor.matmul(lg_ps[:, b, :], x2T[:, k, b * S:(b + 1) * S], gw_sb[:, k, :],
                                          start=(k == 0), stop=(k == KC - 1))
            mm.then_inc(s_lg, 1)

            SHARED = (E - 1) * PIECES * PW

            def shared_up(n):
                for m in range(KC):
                    for half in range(2):
                        if n == 0:
                            pe.wait_ge(s_x2hi, 4)
                        else:
                            pe.wait_ge(s_bb if half else s_aa, m + 1)
                        for k in range(KC):
                            at = SHARED + k * PW + half * F + m * 128
                            terms = ((w_hi, x2T_hi), (w_hi, x2T_lo), (w_lo, x2T_hi))
                            for i, (w, xt) in enumerate(terms):
                                mm = nc.tensor.matmul(bank[2 * m + half][:, 0:HALF], w[:, at:at + 128],
                                                      xt[:, k, n * HALF:(n + 1) * HALF],
                                                      start=(k == 0 and i == 0), stop=(k == KC - 1 and i == 2))
                        mm.then_inc(s_us, 1)

            pe.wait_ge(s_wlo, PIECES * E)
            pe.wait_ge(s_x2lo, 4)
            shared_up(0)
            pe.wait_ge(s_fc, 4)
            pe.wait_ge(s_hot, 1)
            nc.tensor.matmul(pos_ps, before[:, :], both[:, B:, :], start=True, stop=False)
            for back in range(1, B):
                mm = nc.tensor.matmul(pos_ps, ones_b[:, 0:S], both[:, B - back:2 * B - back, :],
                                      start=False, stop=(back == B - 1))
            mm.then_inc(s_pos, 1)
            for b in range(B):
                mm = nc.tensor.matmul(cnt_ps, ones_b[:, :], both[:, B + b, :], start=(b == 0), stop=(b == B - 1))
            mm.then_inc(s_cnt, 1)
            shared_up(1)
            pe.wait_ge(s_tv, 2)
            for kb in range(TOP * B):
                mm = nc.tensor.matmul(map_ps, slot_hot[:, kb, :], tile_val[:, kb, :, :],
                                      start=(kb == 0), stop=(kb == TOP * B - 1))
            mm.then_inc(s_map, 1)
            pe.wait_ge(s_te, 1)
            for p in range(B // 2):
                pe.wait_ge(s_gsl, 2 * (p // 2 + 1))
                if p >= 2:
                    pe.wait_ge(s_yse, p - 1)
                for b in (2 * p, 2 * p + 1):
                    ps = ye_ps[p % 2][0:S, (b % 2) * D:(b % 2 + 1) * D]
                    t = slice(b * S, (b + 1) * S)
                    for k in range(KC):
                        at = SHARED + KC * PW + k * D
                        terms = ((gs_hi, w_hi), (gs_hi, w_lo), (gs_lo, w_hi))
                        for i, (g, w) in enumerate(terms):
                            mm = nc.tensor.matmul(ps, g[:, k, t], w[:, at:at + D],
                                                  start=(k == 0 and i == 0), stop=(k == KC - 1 and i == 2))
                mm.then_inc(s_ys, 1)

            def split_product(ps, par, sel, parts_hi, parts_lo, col, width, bias_at):
                nc.tensor.matmul(ps, sel[:, par, :].to_broadcast([128, 128]), bias[:, bias_at:bias_at + width],
                                 start=True, stop=False)
                for k in range(KC):
                    rh = w_hi[:, bass.ds(col + k * width, width)]
                    rl = w_lo[:, bass.ds(col + k * width, width)]
                    nc.tensor.matmul(ps, parts_hi[:, par, k, :], rh, start=False, stop=False)
                    nc.tensor.matmul(ps, parts_hi[:, par, k, :], rl, start=False, stop=False)
                    mm = nc.tensor.matmul(ps, parts_lo[:, par, k, :], rh, start=False, stop=(k == KC - 1))
                return mm

            def turn_x(t, n, first):
                par = n % 2
                pe.wait_ge(s_xg[n], (t // XG + 1) * 16)
                if not first:
                    pe.wait_ge(s_xtl, t - 1)
                for k in range(KC):
                    mm = nc.tensor.transpose(xt_ps[par][:, k, :], xg[:, n, k * 128:(k + 1) * 128], ident[:, :])
                mm.then_inc(s_xtp, 1)

            def up(t, par, col, first):
                pe.wait_ge(s_xtl, t + 1)
                if not first:
                    pe.wait_ge(s_gg, t - 1)
                split_product(h_ps[par][:, :], par, sel_up, xT_hi, xT_lo, col, 2 * F, 0).then_inc(s_h, 1)

            def turn_g(t, par, first):
                pe.wait_ge(s_gg, t + 1)
                if not first:
                    pe.wait_ge(s_gtl, t - 1)
                for k in range(2):
                    mm = nc.tensor.transpose(gt_ps[par][:, k, :], gg[:, par, k * 128:(k + 1) * 128], ident[:, :])
                mm.then_inc(s_gt, 1)

            def down(t, par, col, first):
                pe.wait_ge(s_gtl, t + 1)
                if not first:
                    pe.wait_ge(s_yo, t - 1)
                split_product(ye_ps[par][:, 0:D], par, sel_down, gT_hi, gT_lo, col + 2 * PW, D, 2 * F).then_inc(s_ye, 1)

            def column(t):
                e = pe.value_load(tile_ei[0:1, bass.ds(t, 1)], min_val=0, max_val=ER - 1)
                return e * (PIECES * PW)

            def tile_step(t, n, first=False, second=False, third=False, more=True):
                par = n % 2
                if more:
                    turn_x(t + 1, (n + 1) % XG, first)
                up(t, par, column(t), first or second)
                if not first:
                    turn_g(t - 1, 1 - par, second or third)
                if third:
                    pe.wait_ge(s_yse, B // 2)
                if not (first or second):
                    down(t - 2, par, column(t - 2), third)

            pe.wait_ge(s_bias, 32)
            pe.wait_ge(s_te, 2)
            pe.wait_ge(s_idx, 1)
            turn_x(0, 0, True)
            tile_step(0, 0, first=True)
            tile_step(1, 1, second=True)
            tile_step(2, 2, third=True)
            tile_step(3, 3)
            with pe.Fori(XG, NT - 1, XG) as t:
                for n in range(XG):
                    tile_step(t + n, n)
            tile_step(NT - 1, 0, more=False)
            turn_g(NT - 1, 0, False)
            down(NT - 2, 1, column(NT - 2), False)
            down(NT - 1, 0, column(NT - 1), False)

        @block.scalar
        def _(act):
            act.dma_start(wk_sb[:, :, :], wkT).then_inc(s_wk, 16)
            for n in range(2):
                act.dma_start(ctxT_sb[:, :, n * HALF:(n + 1) * HALF], ctxT[:, :, n * HALF:(n + 1) * HALF])\
                    .then_inc(s_ctx[n], 16)
            nc.scalar.preload_act_table(ACT.Sqrt)
            act.wait_ge(s_stats, 1)
            nc.scalar.activation(std[:, :], std[:, :], ACT.Sqrt).then_inc(s_std, 1)
            act.wait_ge(s_small, 48)
            nc.scalar.activation(tanh_gate[:, :], gate_cols[:, :], ACT.Tanh).then_inc(s_tg, 1)

            def take_keys(n):
                for m in range(KC):
                    act.wait_ge(s_k, 2 * n + m + 1)
                    nc.scalar.activation(kT[:, m, n * HALF:(n + 1) * HALF], bank[2 * n + m][:, 0:HALF], ACT.Identity,
                                         bias=bqk_sb[:, 1, m:m + 1]).then_inc(s_kt, 1)

            def take_xhatT(n):
                act.wait_ge(s_xt, n + 1)
                if n:
                    act.wait_ge(s_q, KC)
                for k in range(KC):
                    nc.scalar.activation(xhatT[:, k, :], bank[2 * n + 2 + k][:, 0:HALF],
                                         ACT.Copy).then_inc(s_xts, 1)

            def take_qT(n):
                for m in range(KC):
                    act.wait_ge(s_q, 2 * n + m + 1)
                    nc.scalar.activation(qT[:, m, n * HALF:(n + 1) * HALF], bank[4 - 2 * n + m][:, 0:HALF],
                                         ACT.Identity, bias=bqk_sb[:, 0, m:m + 1]).then_inc(s_qt, 1)

            def take_queries(b, k, first=False):
                if not first:
                    act.wait_ge(s_sc, NG * (b - 1) + 2 * k + 2)
                nc.scalar.activation(q_now[:, k, :], qT[:, k, bass.ds(b * S, S)], ACT.Copy).then_inc(s_qn[k], 1)

            def take_values(b):
                for par in range(2):
                    ins = nc.scalar.activation(
                        v_pad[:, :, par, par, :],
                        v_sb[:, bass.ds(b, 1), :].rearrange("p o (a q d) -> p (o a) q d", q=2, d=HD)[:, :, par, :],
                        ACT.Copy)
                ins.then_inc(s_vp, 1)

            def exps(b, g, first):
                act.wait_ge(s_sh, NG * b + g + 1)
                if not first:
                    act.wait_ge(s_pt, NG * (b - 1) + g + 1)
                    act.wait_ge(s_sum, NG * (b - 1) + g + 1)
                nc.scalar.activation(probs[:, g, :, :], sc_sb[:, g % 2, :, :], ACT.Exp, scale=HD ** -0.5)\
                    .then_inc(s_ex, 1)

            def take_pT(b, g, first):
                act.wait_ge(s_pt, NG * b + g + 1)
                if not (first and g < 2):
                    act.wait_ge(s_pv, NG * b + g - 1)
                nc.scalar.activation(pT_sb[:, g % 2, :, :], pT_ps[g % 2], ACT.Copy).then_inc(s_pts, 1)

            def round_weights(e, j):
                act.wait_ge(s_raw[j], 16 * (e + 1))
                nc.scalar.activation(w_hi[:, bass.ds(PW * (PIECES * e + j), PW)], raw[:, j, :], ACT.Copy)\
                    .then_inc(s_whi, 1)

            def take_rT(b, first):
                act.wait_ge(s_rt, b + 1)
                if not first:
                    act.wait_ge(s_on, b)
                nc.scalar.activation(rT_sb[:, :, :], rT_ps, ACT.Copy).then_inc(s_rts, 1)

            def attend(i, now=True, before=True, more=True, first=False, second=False):
                for g in range(NG):
                    if before:
                        take_pT(i - 1, g, second)
                    if g == NG - 1 and before:
                        take_rT(i - 1, second)
                    if g == 0 and before:
                        exps(i - 1, NG - 1, second)
                    if g and now:
                        exps(i, g - 1, first)
                    if g >= 2 and more:
                        take_queries(i + 1, g - 2)
                    if g < PIECES:
                        round_weights(i, g)
                if before:
                    act.wait_ge(s_pv, NG * i)
                if now:
                    take_values(i)

            take_keys(0)
            take_xhatT(0)
            take_qT(0)
            act.wait_ge(s_qt, KC)
            for k in range(KC):
                take_queries(0, k, first=True)
            take_keys(1)
            exps(0, 0, True)
            round_weights(0, 0)
            take_xhatT(1)
            exps(0, 1, True)
            round_weights(0, 1)
            take_queries(1, 0)
            take_qT(1)
            exps(0, 2, True)
            round_weights(0, 2)
            take_queries(1, 1)
            act.wait_ge(s_vs, B // 2)
            act.wait_ge(s_const, 5)
            act.wait_ge(s_qt, 2 * KC)
            take_values(0)
            attend(1, second=True)
            with act.Fori(2, B - 1) as i:
                attend(i)
            attend(B - 1, more=False)
            attend(B, now=False, more=False)

            nc.scalar.preload_act_table(ACT.Sqrt)
            act.wait_ge(s_stats, 2)
            nc.scalar.activation(std[:, :], std[:, :], ACT.Sqrt).then_inc(s_std, 1)
            nc.scalar.preload_act_table(ACT.Exp)
            for n in range(2):
                act.wait_ge(s_x2t, n + 1)
                for k in range(KC):
                    src, at = bank[2 * n + k][:, 0:HALF], slice(n * HALF, (n + 1) * HALF)
                    nc.scalar.activation(x2T[:, k, at], src, ACT.Copy).then_inc(s_x2t32, 1)
                for k in range(KC):
                    src, at = bank[2 * n + k][:, 0:HALF], slice(n * HALF, (n + 1) * HALF)
                    nc.scalar.activation(x2T_hi[:, k, at], src, ACT.Copy).then_inc(s_x2hi, 1)
            act.wait_ge(s_b, 48)
            nc.scalar.activation(b1s_half[:, :], b1s[:, 0:KC], ACT.Copy, scale=0.5).then_inc(s_tha, 1)
            act.wait_ge(s_gexp, 1)
            nc.scalar.activation(pg[:, :, :], pg[:, :, :], ACT.Exp).then_inc(s_gexp, 1)
            act.wait_ge(s_tha, 1)
            def shared_parts(t):
                m, a, b, u = t % 2, a_sh[t % 2], b_sh[t % 2], u_sh[t % 2]
                act.wait_ge(s_us, 2 * t + 1)
                if t == 1:
                    act.wait_ge(s_xr, 32)
                if t >= 2:
                    act.wait_ge(s_gs, t - 1)
                nc.scalar.activation(b, bank[2 * m][:, 0:HALF], ACT.Tanh, bias=b1s_half[:, m:m + 1],
                                     scale=0.5).then_inc(s_tha, 1)
                nc.scalar.activation(a, bank[2 * m][:, 0:HALF], ACT.Identity, bias=b1s_half[:, m:m + 1],
                                     scale=0.5)
                act.wait_ge(s_tha, t + 2)
                nc.scalar.activation(u, b, ACT.Copy, bias=1.0).then_inc(s_aa, 1)
                act.wait_ge(s_us, 2 * t + 2)
                act.wait_ge(s_aa, t + 1)
                nc.scalar.activation(b, bank[2 * m + 1][:, 0:HALF], ACT.Identity,
                                     bias=b1s[:, KC + m:KC + m + 1]).then_inc(s_bb, 1)

            def shared_high(t):
                m, at = t % 2, slice(t // 2 * HALF, (t // 2 + 1) * HALF)
                act.wait_ge(s_gs, t + 1)
                nc.scalar.activation(gs_hi[:, m, at], g_sh[:, m, at], ACT.Copy).then_inc(s_gsh, 1)

            shared_parts(0)
            for t in range(1, 4):
                shared_parts(t)
                shared_high(t - 1)
            shared_high(3)

            def take_x(t, par, first):
                act.wait_ge(s_xtp, t + 1)
                if not first:
                    act.wait_ge(s_h, t - 1)
                nc.scalar.activation(xT_hi[:, par, :, :], xt_ps[par], ACT.Copy).then_inc(s_xth, 1)

            def tanh_a(t, par, first):
                act.wait_ge(s_h, t + 1)
                if not first:
                    act.wait_ge(s_ug, t - 1)
                nc.scalar.activation(th[:, par, :], h_ps[par][:, 0:F], ACT.Tanh, scale=0.5).then_inc(s_th, 1)

            def take_g(t, par, first):
                act.wait_ge(s_gt, t + 1)
                if not first:
                    act.wait_ge(s_ye, t - 1)
                nc.scalar.activation(gT_hi[:, par, :, :], gt_ps[par], ACT.Copy).then_inc(s_gth, 1)

            def weigh(t, par, first):
                act.wait_ge(s_ye, t + 1)
                if not first:
                    act.wait_ge(s_yw[par], (t // 2) * 16)
                nc.scalar.activation(ye[:, par, :], ye_ps[par][:, 0:D], ACT.Copy, scale=slot_w[:, bass.ds(t, 1)])\
                    .then_inc(s_yo, 1)

            def tile_step(t, par, first=False, second=False, third=False, fourth=False, more=True, now=True):
                if now:
                    if more:
                        take_x(t + 1, 1 - par, first)
                    tanh_a(t, par, first or second)
                if not first:
                    take_g(t - 1, 1 - par, second or third)
                if not (first or second):
                    weigh(t - 2, par, third or fourth)

            act.wait_ge(s_idx, 1)
            act.wait_ge(s_bias, 32)
            take_x(0, 0, True)
            tile_step(0, 0, first=True)
            tile_step(1, 1, second=True)
            tile_step(2, 0, third=True)
            tile_step(3, 1, fourth=True)
            with act.Fori(4, NT - 1, 2) as t:
                tile_step(t, 0)
                tile_step(t + 1, 1)
            tile_step(NT - 1, 0, more=False)
            tile_step(NT, 1, now=False)
            weigh(NT - 1, 0, False)

        @block.vector
        def _(dve):
            def norm(src, dst, times):
                for b in range(B):
                    if times == 0:
                        if b % (B // 2) == 0:
                            dve.wait_ge(s_x[b // (B // 2)], 16)
                        nc.vector.bn_stats(stats[:, b, :], src[:, b, :]).then_inc(s_st, 1)
                for b in range(B):
                    dve.wait_ge(s_st, B * times + b + 1)
                    nc.vector.bn_aggr(meanvar[:, b, :], stats[:, b, :]).then_inc(s_st2, 1)
                dve.wait_ge(s_st2, B * (times + 1))
                nc.vector.tensor_scalar(std[:, :], meanvar[:, :, 1], EPS, None, ALU.add).then_inc(s_stats, 1)
                dve.wait_ge(s_std, times + 1)
                nc.vector.reciprocal(rstd[:, :], std[:, :]).then_inc(s_rstd, 1)
                dve.wait_ge(s_rstd, times + 1)
                for b in range(B):
                    nc.vector.tensor_scalar(dst[:, b, :], src[:, b, :], meanvar[:, b, 0:1], rstd[:, b:b + 1],
                                            ALU.subtract, ALU.mult).then_inc(s_xh, 1)

            norm(x_sb, xhat, 0)
            dve.wait_ge(s_small, 48)

            def add_bv(p):
                dve.wait_ge(s_v, p + 1)
                nc.vector.tensor_tensor(v_sb[:, 2 * p:2 * p + 2, :], grid(bank[6 + p % 2], S, 2, D),
                                        bvo_sb[:, 0:1, :].to_broadcast([S, 2, D]), ALU.add).then_inc(s_vs, 1)

            def mask_scores(g):
                for h in range(G):
                    ins = nc.vector.tensor_tensor_reduce(
                        out=sc_sb[:, g % 2, h, :], in0=sc_ps[g % 2][:, h, :], in1=mask[:, :], scale=1.0,
                        scalar=LEAST, op0=ALU.add, op1=ALU.max, accum_out=rowmax[:, g % 2, h:h + 1])
                ins.then_inc(s_mk, 1)

            def sum_probs(b, g):
                dve.wait_ge(s_ex, NG * b + g + 1)
                nc.vector.tensor_reduce(sums[:, G * g:G * g + G], probs[:, g, :, :], AX.X, ALU.add)\
                    .then_inc(s_sum, 1)

            def recip_sums(b, first):
                dve.wait_ge(s_sum, NG * (b + 1))
                nc.vector.reciprocal(rsum[:, :], sums[:, :]).then_inc(s_rs, 1)
                dve.wait_ge(s_rs, b + 1)
                if not first:
                    dve.wait_ge(s_rt, b)
                nc.vector.tensor_copy(rexp[:, :, :], rsum[:, :].unsqueeze(2).to_broadcast([S, HEADS, HD]))\
                    .then_inc(s_re, 1)

            def norm_outputs(b, first):
                dve.wait_ge(s_rts, b + 1)
                dve.wait_ge(s_pv, NG * (b + 1))
                if not first:
                    dve.wait_ge(s_y, b)
                nc.vector.tensor_tensor(oT_sb[:, :, :], oT_ps, rT_sb[:, :, :], ALU.mult).then_inc(s_on, 1)

            def residual(b):
                at = bass.ds(b, 1)
                dve.wait_ge(s_y, b + 1)
                nc.vector.tensor_tensor(y_sb[:, :], y_ps, bvo_sb[:, 1, :], ALU.add).then_inc(s_yb, 1)
                dve.wait_ge(s_yb, b + 1)
                xb = x_sb[:, at, :].rearrange("p o d -> p (o d)")
                nc.vector.scalar_tensor_tensor(out=xb, in0=y_sb[:, :], scalar=tanh_gate[0:S, 0:1], in1=xb,
                                               op0=ALU.mult, op1=ALU.add).then_inc(s_x2, 1)
                dve.wait_ge(s_x2, b + 1)
                nc.vector.bn_stats(stats[:, at, :].rearrange("p o d -> p (o d)"), xb).then_inc(s_st, 1)

            def attend(i, now=True, before=True, last=True, first=False, second=False):
                for g in range(NG):
                    if now:
                        dve.wait_ge(s_sc, NG * i + g + 1)
                    if now and g >= 2:
                        sum_probs(i, g - 2)
                    elif before and g < 2:
                        sum_probs(i - 1, g + 2)
                    if now:
                        mask_scores(g)
                    if g == 1 and before:
                        recip_sums(i - 1, second)
                    if g == 2 and last:
                        residual(i - 2)
                if before:
                    norm_outputs(i - 1, second)

            dve.wait_ge(s_tg, 1)
            dve.wait_ge(s_const, 4)
            for g in range(NG):
                if g < 2:
                    add_bv(g)
                dve.wait_ge(s_sc, g + 1)
                if g >= 2:
                    sum_probs(0, g - 2)
                mask_scores(g)
            add_bv(2)
            add_bv(3)
            attend(1, last=False, second=True)
            with dve.Fori(2, B) as i:
                attend(i)
            attend(B, now=False)
            residual(B - 1)

            norm(x_sb, x2n, 1)
            dve.wait_ge(s_b, 48)
            nc.vector.tensor_copy(b_hi[:, :], b_raw[:, :]).then_inc(s_brow, 1)
            dve.wait_ge(s_brow, 1)
            nc.vector.tensor_tensor(b_lo[:, :], b_raw[:, :], b_hi[:, :], ALU.subtract).then_inc(s_brow, 1)

            steps = [0]

            def step(ins):
                steps[0] += 1
                ins.then_inc(s_chain, 1)
                dve.wait_ge(s_chain, steps[0])

            def over_e(t):
                return t.unsqueeze(2).to_broadcast([S, B, ER])

            dve.wait_ge(s_fc, 4)
            dve.wait_ge(s_gl, 32)
            dve.wait_ge(s_lg, 1)
            step(nc.vector.tensor_tensor(pg[:, :, :], lg_ps, gb_sb[:, :].unsqueeze(1).to_broadcast([S, B, ER]), ALU.add))
            step(nc.vector.tensor_reduce(gsum[:, :], pg[:, :, :], AX.X, ALU.max))
            nc.vector.tensor_tensor(pg[:, :, :], pg[:, :, :], over_e(gsum[:, :]), ALU.subtract).then_inc(s_gexp, 1)
            dve.wait_ge(s_gexp, 2)
            step(nc.vector.tensor_reduce(gsum[:, :], pg[:, :, :], AX.X, ALU.add))
            step(nc.vector.reciprocal(first[:, :], gsum[:, :]))
            step(nc.vector.tensor_tensor(pg[:, :, :], pg[:, :, :], over_e(first[:, :]), ALU.mult))
            for n in range(2):
                p = pg if n == 0 else pg2
                step(nc.vector.tensor_reduce(top[:, n, :], p[:, :, :], AX.X, ALU.max))
                step(nc.vector.tensor_tensor(eq[:, :, :], p[:, :, :], over_e(top[:, n, :]), ALU.is_equal))
                step(nc.vector.scalar_tensor_tensor(out=eq[:, :, :], in0=eq[:, :, :], scalar=-float(ER),
                                                    in1=iota8[:, :, :], op0=ALU.mult, op1=ALU.add))
                step(nc.vector.tensor_reduce(first[:, :], eq[:, :, :], AX.X, ALU.min))
                step(nc.vector.tensor_tensor(hot[:, n, :, :], eq[:, :, :], over_e(first[:, :]), ALU.is_equal))
                if n == 0:
                    step(nc.vector.scalar_tensor_tensor(out=pg2[:, :, :], in0=hot[:, 0, :, :], scalar=-4.0,
                                                        in1=pg[:, :, :], op0=ALU.mult, op1=ALU.add))
            dve.wait_ge(s_fc, 4)
            nc.vector.tensor_tensor(both[:, B:, :], hot[:, 0, :, :], hot[:, 1, :, :], ALU.add).then_inc(s_hot, 1)
            KB = TOP * B
            top16 = top[:, :, :].rearrange("p k b -> p (k b)")
            step(nc.vector.tensor_copy(top_hi[:, :], top16))
            nc.vector.tensor_copy(vals[:, :, 2], top_hi[:, :].bitcast(F32))
            nc.vector.tensor_tensor(vals[:, :, 3], top16, top_hi[:, :].bitcast(F32), ALU.subtract)
            step(nc.vector.tensor_scalar(late[:, 0:1], row8[:, :], ER - 0.5, -float(ER), ALU.is_ge, ALU.mult))
            step(nc.vector.tensor_tensor(row8[:, :], row8[:, :], late[:, 0:1], ALU.add))
            dve.wait_ge(s_cnt, 1)
            step(nc.vector.tensor_tensor(cnt_gt[:, :, :], iota_j[:, :, :],
                                         cnt_ps.unsqueeze(2).to_broadcast([128, ER, 7]), ALU.is_lt))
            step(nc.vector.tensor_reduce(tiles[:, :], cnt_gt[:, :, :], AX.X, ALU.add))
            step(nc.vector.tensor_tensor(t_less[:, :, :], less[:, :, :],
                                         tiles[:, :].unsqueeze(1).to_broadcast([128, ER, ER]), ALU.mult))
            step(nc.vector.tensor_reduce(tile0[:, :], t_less[:, :, :], AX.X, ALU.add))
            dve.wait_ge(s_pos, 1)
            step(nc.vector.scalar_tensor_tensor(out=slots[:, :, :],
                                                in0=tile0[0:S, :].unsqueeze(1).to_broadcast([S, B, ER]),
                                                scalar=float(PART), in1=pos_ps, op0=ALU.mult, op1=ALU.add))
            for k in range(TOP):
                last = nc.vector.tensor_tensor(slot_e[:, k, :, :], hot[:, k, :, :], slots[:, :, :], ALU.mult)
            step(last)
            step(nc.vector.tensor_reduce(slot[:, :], slot_e[:, :, :, :].rearrange("p k b e -> p (k b) e"), AX.X, ALU.add))
            step(nc.vector.tensor_scalar(slot_ti[:, :], slot[:, :], PART / 2 - 0.5, 1.0 / PART, ALU.subtract, ALU.mult))
            step(nc.vector.tensor_copy(slot_t[:, :], slot_ti[:, :]))
            step(nc.vector.scalar_tensor_tensor(out=slot_p[:, :], in0=slot_t[:, :], scalar=-float(PART),
                                                in1=slot[:, :], op0=ALU.mult, op1=ALU.add))
            step(nc.vector.tensor_tensor(eq_t[:, :, :], iota_tok[:, :].unsqueeze(1).to_broadcast([S, KB, NT]),
                                         slot_t[:, :].unsqueeze(2).to_broadcast([S, KB, NT]), ALU.is_equal))
            nc.vector.tensor_tensor(tile_val[:, :, :, :], eq_t[:, :, :].unsqueeze(2).to_broadcast([S, KB, NV, NT]),
                                    vals[:, :, :].unsqueeze(3).to_broadcast([S, KB, NV, NT]), ALU.mult).then_inc(s_tv, 1)
            nc.vector.tensor_tensor(slot_hot[:, :, :], iota_p[:, :].unsqueeze(1).to_broadcast([S, KB, PART]),
                                    slot_p[:, :].unsqueeze(2).to_broadcast([S, KB, PART]), ALU.is_equal).then_inc(s_tv, 1)
            def shared_low(t):
                m, at = t % 2, slice(t // 2 * HALF, (t // 2 + 1) * HALF)
                dve.wait_ge(s_gsh, t + 1)
                nc.vector.tensor_tensor(gs_lo[:, m, at], g_sh[:, m, at], gs_hi[:, m, at], ALU.subtract)\
                    .then_inc(s_gsl, 1)

            step(nc.vector.tensor_tensor(t_ge[:, :, :], iota_t[:, :, :],
                                         tile0[:, :].unsqueeze(1).to_broadcast([128, NT, ER]), ALU.is_ge))
            step(nc.vector.tensor_reduce(tile_e[:, :], t_ge[:, :, :], AX.X, ALU.add))
            step(nc.vector.tensor_scalar(tile_e[:, :], tile_e[:, :], -1.0, None, ALU.add))
            nc.vector.tensor_copy(tile_ei[0:1, 0:NT], tile_e[0:1, :]).then_inc(s_te, 1)
            nc.vector.tensor_scalar(e_hot[:, 0:NT], tile_e[:, :], row8[:, 0:1], None, ALU.is_equal).then_inc(s_te, 1)
            shared_low(0)
            shared_low(1)
            dve.wait_ge(s_map, 1)
            step(nc.vector.tensor_copy(smap[:, :, :], map_ps))
            nc.vector.tensor_tensor(slot_w[:, 0:NT], smap[:, 2, :], smap[:, 3, :], ALU.add)
            nc.vector.tensor_scalar(late[:, :], smap[:, 1, :], TOK - 0.5, -float(TOK), ALU.is_ge, ALU.mult)
            step(nc.vector.scalar_tensor_tensor(out=empty[:, :], in0=smap[:, 0, :], scalar=1.0, in1=dump[:, :],
                                                op0=ALU.subtract, op1=ALU.mult))
            nc.vector.tensor_tensor(tok_i[:, 0:NT], late[:, :], smap[:, 1, :], ALU.add)
            nc.vector.tensor_tensor(row_i[:, 0:NT], empty[:, :], smap[:, 1, :], ALU.add).then_inc(s_idx, 1)

            shared_low(2)
            shared_low(3)
            dve.wait_ge(s_xr, 32)
            for p in range(B // 2):
                dve.wait_ge(s_ys, p + 1)
                nc.vector.tensor_tensor(acc[:, 2 * p:2 * p + 2, :], grid(ye_ps[p % 2], S, 2, D),
                                        b2s[:, :].unsqueeze(1).to_broadcast([S, 2, D]), ALU.add).then_inc(s_yse, 1)

            dve.wait_ge(s_yse, B // 2)

            def add_shared(b):
                at = bass.ds(b * D, D)
                nc.vector.scalar_tensor_tensor(out=x_flat[:, at], in0=x2n_all[0:S, at], scalar=tanh_gate[0:S, 1:2],
                                               in1=x_flat[:, at], op0=ALU.mult, op1=ALU.add).then_inc(s_xs, 1)

            def take_x(t, par, first):
                if not first:
                    dve.wait_ge(s_h, t - 1)
                nc.vector.tensor_copy(sel_up[:, par, :], e_hot[:, bass.ds(t, 1)])
                dve.wait_ge(s_xth, t + 1)
                nc.vector.tensor_tensor(xT_lo[:, par, :, :], xt_ps[par], xT_hi[:, par, :, :], ALU.subtract)\
                    .then_inc(s_xtl, 1)

            def gate(t, par, first):
                dve.wait_ge(s_th, t + 1)
                nc.vector.scalar_tensor_tensor(out=ug[:, par, :], in0=th[:, par, :], scalar=1.0,
                                               in1=h_ps[par][:, 0:F], op0=ALU.add, op1=ALU.mult).then_inc(s_ug, 1)
                dve.wait_ge(s_ug, t + 1)
                if not first:
                    dve.wait_ge(s_gt, t - 1)
                nc.vector.scalar_tensor_tensor(out=gg[:, par, :], in0=ug[:, par, :], scalar=0.5,
                                               in1=h_ps[par][:, F:2 * F], op0=ALU.mult, op1=ALU.mult).then_inc(s_gg, 1)

            def take_g(t, par, first=False):
                if not first:
                    dve.wait_ge(s_ye, t - 1)
                nc.vector.tensor_copy(sel_down[:, par, :], e_hot[:, bass.ds(t, 1)])
                dve.wait_ge(s_gth, t + 1)
                nc.vector.tensor_tensor(gT_lo[:, par, :, :], gt_ps[par], gT_hi[:, par, :, :], ALU.subtract)\
                    .then_inc(s_gtl, 1)

            def tile_step(t, par, first=False, second=False, third=False, more=True):
                if more:
                    take_x(t + 1, 1 - par, first)
                gate(t, par, first or second)
                if not first:
                    take_g(t - 1, 1 - par, second or third)

            dve.wait_ge(s_bias, 32)
            take_x(0, 0, True)
            tile_step(0, 0, first=True)
            tile_step(1, 1, second=True)
            tile_step(2, 0, third=True)
            tile_step(3, 1)
            assert (NT - 5) // 2 == B
            with dve.Fori(4, NT - 1, 2) as t:
                tile_step(t, 0)
                tile_step(t + 1, 1)
                add_shared(t // 2 - 2)
            tile_step(NT - 1, 0, more=False)
            take_g(NT - 1, 0)
            dve.wait_ge(s_xs, B)
            for b in range(B):
                dve.wait_ge(s_yback[b], 16)
                nc.vector.tensor_tensor(acc[:, b, :], y_back[:, 0, b, :], y_back[:, 1, b, :], ALU.add)\
                    .then_inc(s_rsum, 1)
                dve.wait_ge(s_rsum, b + 1)
                nc.vector.scalar_tensor_tensor(out=acc[:, b, :], in0=acc[:, b, :], scalar=tanh_gate[0:S, 1:2],
                                               in1=x_sb[:, b, :], op0=ALU.mult, op1=ALU.add).then_inc(s_fin, 1)


def kernel(**inputs):
    import numpy as np
    import concourse.bacc as bacc
    from concourse.bass_utils import run_bass_kernel_spmd

    def rows(a):
        return np.ascontiguousarray(a.reshape(KC, 128, -1).transpose(1, 0, 2))

    a = {k: np.asarray(v) for k, v in inputs.items()}
    w1 = np.concatenate([a["L0_ffn_rw1"], a["L0_ffn_sw1"]])
    w2 = np.concatenate([a["L0_ffn_rw2"], a["L0_ffn_sw2"]])
    w1 = w1.reshape(E, KC, 128, 2 * F)
    w2 = w2.reshape(E, 1, KC, 128, D).transpose(0, 1, 3, 2, 4).reshape(E, 1, 128, KC * D)
    ctx = a["ctx_1024"][:, :S, :].transpose(2, 0, 1).reshape(D, TOK)
    arrays = {
        "x": np.ascontiguousarray(a["x"].transpose(1, 0, 2)),
        "ctxT": rows(ctx),
        "wqT": rows(a["L0_xattn_Wq"].T), "wkT": rows(a["L0_xattn_Wk"].T),
        "wvT": rows(a["L0_xattn_Wv"].T), "woT": rows(a["L0_xattn_Wo"].T),
        "bqk": np.ascontiguousarray(np.stack([a["L0_xattn_bq"], a["L0_xattn_bk"]]).reshape(2, KC, 128).transpose(2, 0, 1)),
        "bvo": np.stack([a["L0_xattn_bv"], a["L0_xattn_bo"]]),
        "gates": np.concatenate([a["g_xattn"], a["g_ffn"]]),
        "gate_w": rows(a["L0_ffn_gate_w"]),
        "gate_b": a["L0_ffn_gate_b"],
        "w_all": np.ascontiguousarray(np.concatenate([w1, w2], axis=1).reshape(E * PIECES, 128, PW)),
        "b_routed": np.ascontiguousarray(np.concatenate([a["L0_ffn_rb1"], a["L0_ffn_rb2"]], axis=1)),
        "b1_shared": np.ascontiguousarray(a["L0_ffn_sb1"].reshape(2 * KC, 128).T),
        "b2_shared": a["L0_ffn_sb2"].reshape(D),
    }
    nc = bacc.Bacc("TRN2", target_bir_lowering=False, num_devices=1)
    aps = [nc.dram_tensor(f"in_{n}", v.shape, F32, kind="ExternalInput").ap() for n, v in arrays.items()]
    out = nc.dram_tensor("out", (B, S, D), F32, kind="ExternalOutput").ap()
    block_kernel(nc, *aps, out)
    r = run_bass_kernel_spmd(nc, [{f"in_{n}": v for n, v in arrays.items()}], core_ids=[0])
    return r.results[0]["out"]
```

```python
from contextlib import ExitStack

import concourse.bass as bass
from concourse import mybir

BF16 = mybir.dt.bfloat16
I32 = mybir.dt.int32
U32 = mybir.dt.uint32
F32 = mybir.dt.float32
F32R = mybir.dt.float32r
ALU = mybir.AluOpType
ACT = mybir.ActivationFunctionType
AX = mybir.AxisListType

B, S, D = 8, 112, 256
HEADS, HD = 16, 16
KC = D // 128
TOK = B * S
HALF = TOK // 2
G = 4
NG = HEADS // G
E = 9
ER = 8
F = 256
PIECES = 3
PW = 512
EPS = 1e-5
NEG = -1e30
LEAST = -3e38
PART = 128
TOP = 2
NT = TOP * TOK // PART + ER - 1
POOL_SUMS = (0, 3, 6)
XG = 4
NV = 4


def block_kernel(nc, x, ctxT, wqT, wkT, wvT, woT, bqk, bvo, gates, gate_w, gate_b, w_all, b_routed,
                 b1_shared, b2_shared, out):
    with ExitStack() as ctx:
        def sb(name, shape, dt=F32, scope=ctx):
            return scope.enter_context(nc.sbuf_tensor(name, shape, dt))

        def sem(name):
            return ctx.enter_context(nc.semaphore(name))

        x_sb = sb("x_sb", [S, B, D])
        w_hi = sb("w_hi", [128, E * PIECES * PW], F32R)
        w_lo = sb("w_lo", [128, E * PIECES * PW], F32R)
        ident = sb("ident", [128, 128])
        gate_cols = sb("gate_cols", [128, 2])
        tanh_gate = sb("tanh_gate", [128, 2])
        stats = sb("stats", [S, B, 6])
        meanvar = sb("meanvar", [S, B, 2])
        std = sb("std", [S, B])
        rstd = sb("rstd", [S, B])

        att = ctx.enter_context(ExitStack())
        qT = sb("qT", [128, KC, TOK], scope=att)
        kT = sb("kT", [128, KC, TOK], scope=att)
        wv_sb = sb("wv_sb", [128, KC, D], scope=att)
        wo_sb = sb("wo_sb", [128, KC, D], scope=att)
        bqk_sb = sb("bqk_sb", [128, 2, KC], scope=att)
        bvo_sb = sb("bvo_sb", [S, 2, D], scope=att)
        xhat = sb("xhat", [S, B, D], scope=att)
        v_sb = xhat
        mask = sb("mask", [S, S], scope=att)
        q_now = sb("q_now", [128, KC, S], scope=att)
        k_diag = sb("k_diag", [128, NG, G, 4, S], scope=att)
        v_pad = sb("v_pad", [S, HEADS // 2, 2, 2, HD], scope=att)
        raw = sb("raw", [128, PIECES, PW], scope=att)
        sc_sb = sb("sc_sb", [S, 2, G, S], scope=att)
        rowmax = sb("rowmax", [S, 2, G], scope=att)
        sums = sb("sums", [S, HEADS], scope=att)
        rsum = sb("rsum", [S, HEADS], scope=att)
        probs = sb("probs", [S, NG, G, S], scope=att)
        early = att.enter_context(ExitStack())
        wq_sb = sb("wq_sb", [128, KC, D], scope=early)
        wk_sb = sb("wk_sb", [128, KC, D], scope=early)
        ctxT_sb = sb("ctxT_sb", [128, KC, TOK], scope=early)
        xhatT = sb("xhatT", [128, KC, HALF], scope=early)
        early.close()
        pT_sb = sb("pT_sb", [S, 2, G, S], scope=att)
        rexp = sb("rexp", [S, HEADS, HD], scope=att)
        rT_sb = sb("rT_sb", [128, KC, S], scope=att)
        oT_sb = sb("oT_sb", [128, KC, S], scope=att)
        y_sb = sb("y_sb", [S, D], scope=att)
        att.close()

        x2n_all = sb("x2n", [128, B * D])
        x2n = x2n_all[0:S, :].rearrange("p (b d) -> p b d", b=B)
        gw_sb = sb("gw_sb", [128, KC, ER])
        gb_row = sb("gb_row", [1, ER])
        b1s = sb("b1s", [128, 2 * KC])
        b1s_half = sb("b1s_half", [128, KC])
        b2s = sb("b2s", [S, D])
        bias = sb("bias", [128, 2 * F + D], F32R)
        pg = sb("pg", [S, B, ER])
        pg2 = sb("pg2", [S, B, ER])
        top = sb("top", [S, TOP, B])
        gsum = sb("gsum", [S, B])
        eq = sb("eq", [S, B, ER])
        first = sb("first", [S, B])
        hot = sb("hot", [S, TOP, B, ER])
        both = sb("both", [S, 2 * B, ER], BF16)
        rank = sb("rank", [S, B, ER])
        before = sb("before", [S, S], BF16)
        ones_b = sb("ones_b", [S, 128], BF16)
        iota_j = sb("iota_j", [128, ER, 7])
        less = sb("less", [128, ER, ER])
        iota_t = sb("iota_t", [128, NT, ER])
        iota_tok = sb("iota_tok", [S, NT])
        iota_p = sb("iota_p", [S, PART])
        row8 = sb("row8", [128, 1])
        dump = sb("dump", [128, NT])
        cnt_gt = sb("cnt_gt", [128, ER, 7])
        tiles = sb("tiles", [128, ER])
        t_less = sb("t_less", [128, ER, ER])
        tile0 = sb("tile0", [128, ER])
        tile_e = sb("tile_e", [128, NT])
        tile_col = sb("tile_col", [1, NT + XG], I32)
        e_hot = sb("e_hot", [128, NT + 1], F32R)
        slots = sb("slots", [S, B, ER])
        slot = sb("slot", [S, TOP * B])
        slot_ti = sb("slot_ti", [S, TOP * B], I32)
        slot_t = sb("slot_t", [S, TOP * B])
        slot_p = sb("slot_p", [S, TOP * B])
        vals = sb("vals", [S, TOP * B, NV])
        top_hi = sb("top_hi", [S, TOP * B], F32R)
        slot_w = sb("slot_w", [128, NT + 1])
        late = sb("late", [128, NT])
        empty = sb("empty", [128, NT])
        smap = sb("smap", [128, NV, NT])
        tok_i = sb("tok_i", [128, NT + 1], U32)
        row_i = sb("row_i", [128, NT + 1], U32)
        eq_t = sb("eq_t", [S, TOP * B, NT])
        t_ge = sb("t_ge", [128, NT, ER])
        sel_up = sb("sel_up", [128, 2, 1], F32R)
        sel_down = sb("sel_down", [128, 2, 1], F32R)
        gT_hi = sb("gT_hi", [128, 2, 2, 128], F32R)
        gT_lo = sb("gT_lo", [128, 2, 2, 128], F32R)
        ye = sb("ye", [128, 2, D])
        split_b = ctx.enter_context(ExitStack())
        b_raw = sb("b_raw", [ER, 2 * F + D], scope=split_b)
        b_hi = sb("b_hi", [ER, 2 * F + D], F32R, scope=split_b)
        b_lo = sb("b_lo", [ER, 2 * F + D], F32R, scope=split_b)
        slot_e = sb("slot_e", [S, TOP, B, ER], scope=split_b)
        split_b.close()
        xT_hi = sb("xT_hi", [128, 2, KC, 128], F32R)
        xT_lo = sb("xT_lo", [128, 2, KC, 128], F32R)
        th = sb("th", [128, 2, F])
        ug = sb("ug", [128, 2, F])
        gg = sb("gg", [128, 2, F])
        x_flat = x_sb[:, :, :].rearrange("p b d -> p (b d)")
        acc = x2n

        route = ctx.enter_context(ExitStack())
        x2T_hi = sb("x2T_hi", [128, KC, TOK], F32R, scope=route)
        x2T = sb("x2T", [128, KC, TOK], scope=route)
        x2T_lo = sb("x2T_lo", [128, KC, TOK], F32R, scope=route)
        g_sh = x2T
        gs_hi = sb("gs_hi", [128, KC, TOK], F32R, scope=route)
        gs_lo = sb("gs_lo", [128, KC, TOK], F32R, scope=route)
        abu = sb("abu", [128, 3 * HALF], scope=route)
        a_sh = [abu[:, 0:HALF], x2n_all[:, 0:HALF]]
        b_sh = [abu[:, HALF:2 * HALF], x2n_all[:, HALF:2 * HALF]]
        u_sh = [abu[:, 2 * HALF:3 * HALF], x2n_all[:, 2 * HALF:3 * HALF]]
        slot_hot = sb("slot_hot", [S, TOP * B, PART], F32R, scope=route)
        tile_val = sb("tile_val", [S, TOP * B, NV, NT], F32R, scope=route)
        route.close()
        xg = sb("xg", [128, XG, D])
        y_back = sb("y_back", [S, TOP, B, D])
        x_rows = nc.dram_tensor("x_rows", [TOK, D], F32, kind="Internal").ap()
        y_rows = nc.dram_tensor("y_rows", [TOP * TOK + NT * PART, D], F32, kind="Internal").ap()

        bank = [ctx.enter_context(nc.psum_tensor(f"bank{n}", [128, 512], F32)) for n in range(8)]

        def grid(t, p, n, w):
            return t[0:p, 0:n * w].rearrange("p (n w) -> p n w", n=n)

        sc_ps = [grid(bank[n], S, G, S) for n in (0, 1)]
        pT_ps = [grid(bank[n], S, G, S) for n in (2, 3)]
        oT_ps = grid(bank[4], 128, KC, S)
        rT_ps = grid(bank[5], 128, KC, S)
        y_ps = bank[6][0:S, 0:D]
        h_ps = [bank[n] for n in (0, 1)]
        xt_ps = [grid(bank[n], 128, KC, 128) for n in (2, 3)]
        gt_ps = [grid(bank[n], 128, 2, 128) for n in (6, 7)]
        ye_ps = [bank[n] for n in (4, 5)]
        lg_ps = grid(bank[6], S, B, ER)
        pos_ps = grid(bank[4], S, B, ER)
        cnt_ps = bank[5][:, 0:ER]
        map_ps = grid(bank[7], 128, NV, NT)

        s_wk, s_wv, s_wq, s_bqk, s_bvo, s_gates, s_b, s_wo = (
            sem(n) for n in ("wk_in", "wv_in", "wq_in", "bqk_in", "bvo_in", "gates_in", "biases_in", "wo_in"))
        s_x = [sem(f"x_in{n}") for n in range(2)]
        s_ctx = [sem(f"ctx_in{n}") for n in range(2)]
        s_raw = [sem(f"raw_in{j}") for j in range(PIECES)]
        s_const, s_zero = sem("consts_ready"), sem("zeros_ready")
        s_k, s_kt = sem("k_projected"), sem("kT_ready")
        s_v, s_vs = sem("v_projected"), sem("v_ready")
        s_st2 = sem("meanvars_ready")
        s_st, s_stats, s_std, s_rstd, s_xh = (
            sem("stats_ready"), sem("meanvar_ready"), sem("std_ready"), sem("rstd_ready"), sem("xhat_ready"))
        s_xt, s_xts = sem("xhat_transposed"), sem("xhatT_ready")
        s_q, s_qt = sem("q_projected"), sem("qT_ready")
        s_tg = sem("tanh_gate_ready")
        s_qn = [sem(f"q_now{k}_ready") for k in range(KC)]
        s_vp = sem("v_pad_ready")
        s_kd = [sem(f"k_diag_in{g}") for g in range(NG // 2)]
        s_sc, s_mk, s_sh, s_ex, s_sum = (
            sem("scores_ready"), sem("scores_masked"), sem("scores_shifted"),
            sem("probs_ready"), sem("sums_ready"))
        s_pt, s_pts, s_pv = sem("probs_transposed"), sem("pT_ready"), sem("pv_done")
        s_rs, s_re, s_rt, s_rts = (
            sem("rsum_ready"), sem("rexp_ready"), sem("rsum_transposed"), sem("rT_ready"))
        s_on, s_y, s_yb, s_x2 = sem("oT_ready"), sem("y_projected"), sem("y_biased"), sem("x2_ready")
        s_whi, s_wlo = sem("w_hi_ready"), sem("w_lo_ready")
        s_brow, s_bias = sem("bias_rows_split"), sem("bias_in")
        s_fc = sem("expert_consts_ready")
        s_x2hi, s_x2t32 = sem("x2T_hi_ready"), sem("x2T_ready")
        s_xr, s_hot, s_pos, s_cnt = sem("x_rows_stored"), sem("hot_ready"), sem("pos_ready"), sem("counts_ready")
        s_te = sem("tile_experts_ready")
        s_tv, s_map, s_idx = sem("tile_val_ready"), sem("map_ready"), sem("slot_rows_ready")
        s_slot, s_sw = sem("slots_ready"), sem("slot_weights_ready")
        s_us, s_tha, s_aa, s_bb, s_pu = (
            sem("shared_up"), sem("shared_tanh"), sem("shared_a"), sem("shared_b"), sem("shared_u"))
        s_gs, s_gsh, s_gsl, s_ys, s_yse = (
            sem("shared_g"), sem("shared_g_hi"), sem("shared_g_lo"), sem("shared_y"), sem("shared_y_out"))
        s_xg = [sem(f"x_gathered{n}") for n in range(XG)]
        s_yw = [sem(f"y_scattered{n}") for n in range(2)]
        s_xtp, s_xth, s_xtl = (
            sem("xg_transposed"), sem("xT_hi_ready"), sem("xT_lo_ready"))
        s_xs, s_rsum = sem("shared_added"), sem("routed_summed")
        s_yback = [sem(f"y_back_in{b}") for b in range(B)]
        s_gl = sem("gate_in")
        s_chain = sem("router_step")
        s_x2t, s_x2lo = sem("x2n_transposed"), sem("x2T_lo_ready")
        s_lg = sem("logits_ready")
        s_gexp = sem("gate_exp_ready")
        s_h, s_th, s_ug, s_gg, s_gt, s_gth, s_gtl, s_ye, s_yo = (
            sem("h_ready"), sem("tanh_ready"), sem("u_ready"), sem("g_ready"), sem("g_transposed"),
            sem("gT_hi_ready"), sem("gT_lo_ready"), sem("ye_ready"), sem("ye_weighted"))
        s_psum = sem("pool_routed_summed")
        s_fin, s_out = [sem(f"out_ready{b}") for b in range(B)], sem("out_stored")

        block = ctx.enter_context(nc.Block())

        def head_rows(h):
            return slice(HD * (h % 8), HD * (h % 8) + HD)

        @block.sync
        def _(sp):
            def load_x(n):
                half = slice(n * B // 2, (n + 1) * B // 2)
                sp.dma_start(x_sb[:, half, :], x[:, half, :]).then_inc(s_x[n], 16)

            def load_ctx(n):
                half = slice(n * HALF, (n + 1) * HALF)
                sp.dma_start(ctxT_sb[:, :, half], ctxT[:, :, half]).then_inc(s_ctx[n], 16)

            load_ctx(0)
            load_x(0)
            sp.dma_start(bqk_sb[:, :, :], bqk).then_inc(s_bqk, 16)
            sp.dma_start(wv_sb[:, :, :], wvT).then_inc(s_wv, 16)
            load_x(1)
            sp.dma_start(gate_cols[:, :], gates.partition_broadcast(128)).then_inc(s_gates, 16)
            sp.dma_start(bvo_sb[:, :, :], bvo.partition_broadcast(S)).then_inc(s_bvo, 16)
            load_ctx(1)
            sp.dma_start(wo_sb[:, :, :], woT).then_inc(s_wo, 16)
            for j in range(PIECES):
                sp.dma_start(raw[:, j, :], w_all[j]).then_inc(s_raw[j], 16)

            def load_keys(p, h):
                g = h // G
                sp.dma_start(k_diag[head_rows(h), g::2, h % G, bass.ds(p % 2 * 2, 2), :],
                             kT[head_rows(h), :, bass.ds(p * (2 * S), 2 * S)]).then_inc(s_kd[g], 16)

            def load_weights(e, j):
                sp.wait_ge(s_wlo, PIECES * (e - 1) + j + 1)
                sp.dma_start(raw[:, j, :], w_all[bass.ds(PIECES * e + j, 1)].rearrange("a p n -> (a p) n"))\
                    .then_inc(s_raw[j], 16)

            def load_ahead(p, first=False, more=True):
                for b in range(2):
                    for g in range(NG):
                        if g:
                            load_weights(2 * p + 1 + b, g - 1)
                        if more and b == 0:
                            for h in (2 * g, 2 * g + 1):
                                if h % G == 0:
                                    if not first:
                                        sp.wait_ge(s_sc, NG * (2 * p - 1) + h // G + 3)
                                    sp.wait_ge(s_kd[h // G], 16 * G * (p + 1))
                                load_keys(p + 1, h)

            sp.wait_ge(s_zero, 1)
            sp.wait_ge(s_kt, KC)
            for h in range(HEADS // 2):
                load_keys(0, h)
            load_ahead(0, first=True)
            sp.wait_ge(s_kt, 2 * KC)
            with sp.Fori(1, B // 2 - 1) as p:
                load_ahead(p)
            load_ahead(B // 2 - 1, more=False)
            sp.wait_ge(s_sc, NG * B)
            sp.dma_start(gw_sb[:, :, :], gate_w).then_inc(s_gl, 16)
            sp.dma_start(gb_row[:, :], gate_b).then_inc(s_gl, 16)
            sp.dma_start(b1s[:, :], b1_shared).then_inc(s_b, 16)
            sp.dma_start(b2s[:, :], b2_shared.partition_broadcast(S)).then_inc(s_b, 16)
            sp.wait_ge(s_x2, B)
            sp.wait_ge(s_wlo, PIECES * E)
            sp.dma_start(b_raw[:, :], b_routed).then_inc(s_b, 16)
            for n in range(2):
                half = slice(n * B // 2, (n + 1) * B // 2)
                sp.wait_ge(s_xh, B + (n + 1) * B // 2)
                sp.dma_start(x_rows.rearrange("(b s) d -> s b d", s=S)[:, half, :], x2n[:, half, :])\
                    .then_inc(s_xr, 16)
            sp.wait_ge(s_brow, 2)
            sp.wait_ge(s_fc, 1)
            sp.dma_start(bias[0:ER, :].bitcast(F32), b_hi[:, :].bitcast(F32)).then_inc(s_bias, 16)
            sp.dma_start(bias[ER:2 * ER, :].bitcast(F32), b_lo[:, :].bitcast(F32)).then_inc(s_bias, 16)
            for n in range(2):
                sp.wait_ge(s_yw[n], 16 * ((NT + 1 - n) // 2))
            for b in range(B):
                sp.dma_start(y_back[:, :, b, :],
                             y_rows[0:TOP * TOK, :].rearrange("(k b s) d -> s k b d", k=TOP, s=S)[:, :, b, :])\
                    .then_inc(s_yback[b], 16)
            for b in range(B):
                sp.wait_ge(s_fin[b], 1)
                sp.dma_start(out[b], acc[:, b, :]).then_inc(s_out, 16)
            sp.wait_ge(s_out, 16 * B)

        @block.gpsimd
        def _(pool):
            nc.gpsimd.memset(ident[:, :], 0.0).then_inc(s_const, 1)
            nc.gpsimd.memset(mask[:, :], 0.0).then_inc(s_const, 1)
            pool.wait_ge(s_const, 2)
            nc.gpsimd.affine_select(out=ident[:, :], in_=ident[:, :], compare_op=ALU.not_equal, fill=1.0,
                                    base=0, pattern=[[-1, 128]], channel_multiplier=1).then_inc(s_const, 1)
            nc.gpsimd.affine_select(out=mask[:, :], in_=mask[:, :], compare_op=ALU.is_ge, fill=NEG,
                                    base=0, pattern=[[-1, S]], channel_multiplier=1).then_inc(s_const, 1)
            nc.gpsimd.memset(k_diag[:, :, :, :, :], 0.0).then_inc(s_zero, 1)
            nc.gpsimd.memset(v_pad[:, :, :, :, :], 0.0).then_inc(s_const, 1)

            def split(e, j):
                    at = bass.ds(PW * (PIECES * e + j), PW)
                    pool.wait_ge(s_whi, PIECES * e + j + 1)
                    nc.gpsimd.tensor_tensor(w_lo[:, at], raw[:, j, :], w_hi[:, at], ALU.subtract)\
                        .then_inc(s_wlo, 1)

            def shift(b, g):
                pool.wait_ge(s_mk, NG * b + g + 1)
                nc.gpsimd.tensor_tensor(sc_sb[:, g % 2, :, :], sc_sb[:, g % 2, :, :],
                                        rowmax[:, g % 2, :].unsqueeze(2).to_broadcast([S, G, S]), ALU.subtract)\
                    .then_inc(s_sh, 1)

            with pool.Fori(0, B, 2) as b:
                for n in range(2):
                    for g in range(NG):
                        shift(b + n, g)
                        if g:
                            split(b + n, g - 1)
            for j in range(PIECES):
                split(E - 1, j)
            pool.wait_ge(s_wlo, PIECES * E)
            pool.wait_ge(s_x2, B)
            nc.gpsimd.memset(bias[:, :].bitcast(F32), 0.0).then_inc(s_fc, 1)
            small = dict(allow_small_or_imprecise_dtypes=True)
            nc.gpsimd.iota(rank[:, :, :], pattern=[[0, B], [1, ER]], base=-ER, channel_multiplier=0, **small)
            nc.gpsimd.iota(iota_j[:, :, :], pattern=[[0, ER], [PART, 7]], base=0, channel_multiplier=0, **small)
            nc.gpsimd.iota(iota_t[:, :, :], pattern=[[1, NT], [0, ER]], base=0, channel_multiplier=0, **small)
            nc.gpsimd.iota(iota_tok[:, :], pattern=[[1, NT]], base=0, channel_multiplier=0, **small)
            nc.gpsimd.iota(iota_p[:, :], pattern=[[1, PART]], base=0, channel_multiplier=0, **small)
            nc.gpsimd.iota(row8[:, :], pattern=[[0, 1]], base=0, channel_multiplier=1, **small).then_inc(s_fc, 1)
            nc.gpsimd.iota(dump[:, :], pattern=[[-PART, NT]], base=-TOP * TOK, channel_multiplier=-1, **small)
            nc.gpsimd.iota(vals[:, :, 1], pattern=[[S, TOP * B]], base=0, channel_multiplier=1, **small)
            nc.gpsimd.memset(vals[:, :, 0], 1.0)
            nc.gpsimd.memset(ones_b[:, :], 1.0)
            nc.gpsimd.memset(both[:, 0:B, :], 0.0)
            nc.gpsimd.memset(before[:, :], 1.0)
            nc.gpsimd.memset(less[:, :, :], 1.0).then_inc(s_fc, 1)
            pool.wait_ge(s_fc, 3)
            nc.gpsimd.affine_select(out=before[:, :], in_=before[:, :], compare_op=ALU.is_gt, fill=0.0,
                                    base=0, pattern=[[1, S]], channel_multiplier=-1)
            nc.gpsimd.affine_select(out=less[:, :, :], in_=less[:, :, :], compare_op=ALU.is_gt, fill=0.0,
                                    base=0, pattern=[[1, ER], [-1, ER]], channel_multiplier=0).then_inc(s_fc, 1)

            for n in range(2):
                for k in range(KC):
                    at = slice(n * HALF, (n + 1) * HALF)
                    pool.wait_ge(s_x2t32, 2 * n + k + 1)
                    pool.wait_ge(s_x2hi, 2 * n + k + 1)
                    nc.gpsimd.tensor_tensor(x2T_lo[:, k, at], x2T[:, k, at], x2T_hi[:, k, at], ALU.subtract)\
                        .then_inc(s_x2lo, 1)
            for n in range(2):
                for m in range(KC):
                    t = 2 * n + m
                    a, b, u, at = a_sh[t % 2], b_sh[t % 2], u_sh[t % 2], slice(n * HALF, (n + 1) * HALF)
                    pool.wait_ge(s_aa, t + 1)
                    nc.gpsimd.tensor_tensor(u, u, a, ALU.mult).then_inc(s_pu, 1)
                    pool.wait_ge(s_bb, t + 1)
                    pool.wait_ge(s_pu, t + 1)
                    nc.gpsimd.tensor_tensor(g_sh[:, m, at], u, b, ALU.mult).then_inc(s_gs, 1)

            def gather(t):
                if t >= XG:
                    pool.wait_ge(s_xtp, t - XG + 1)
                nc.gpsimd.indirect_dma_start(
                    xg[:, t % XG, :], None, x_rows, bass.IndirectOffsetOnAxis(ap=tok_i[:, t:t + 1], axis=0),
                    bounds_check=TOK - 1).then_inc(s_xg[t % XG], 16)

            def scatter(t):
                pool.wait_ge(s_yo, t + 1)
                nc.gpsimd.indirect_dma_start(
                    y_rows, bass.IndirectOffsetOnAxis(ap=row_i[:, t:t + 1], axis=0), ye[:, t % 2, :], None,
                    bounds_check=TOP * TOK + NT * PART - 1).then_inc(s_yw[t % 2], 16)

            pool.wait_ge(s_idx, 1)
            pool.wait_ge(s_xr, 32)
            pool.wait_ge(s_us, 8)
            for t in range(NT + XG + 1):
                if t < NT:
                    gather(t)
                if t > XG:
                    scatter(t - XG - 1)
            pool.wait_ge(s_xs, B)
            for n, b in enumerate(POOL_SUMS):
                pool.wait_ge(s_yback[b], 16)
                nc.gpsimd.tensor_tensor(acc[:, b, :], y_back[:, 0, b, :], y_back[:, 1, b, :], ALU.add)\
                    .then_inc(s_psum, 1)
                pool.wait_ge(s_psum, n + 1)
                nc.gpsimd.tensor_tensor(acc[:, b, :], acc[:, b, :], x_sb[:, b, :], ALU.add).then_inc(s_fin[b], 1)

        @block.tensor
        def _(pe):
            def keep_clock(n, ps=bank[7]):
                for _ in range(n):
                    nc.tensor.matmul(ps[:, 0:256], ident[:, :], ident[:, :].unsqueeze(1).to_broadcast([128, 2, 128]),
                                     start=True, stop=True)

            def project(ps, w, rhs, m, n):
                for k in range(KC):
                    last = nc.tensor.matmul(ps[:, 0:HALF], w[:, k, m * 128:(m + 1) * 128],
                                            rhs[:, k, n * HALF:(n + 1) * HALF], start=(k == 0), stop=(k == KC - 1))
                return last

            def keys(n):
                pe.wait_ge(s_ctx[n], 16)
                if n:
                    pe.wait_ge(s_xts, KC)
                for m in range(KC):
                    project(bank[2 * n + m], wk_sb, ctxT_sb, m, n).then_inc(s_k, 1)

            def turn_xhat(n):
                for b in range(4 * n, 4 * n + 4):
                    pe.wait_ge(s_xh, b + 1)
                    for k in range(KC):
                        mm = nc.tensor.transpose(bank[2 * n + 2 + k][:, (b % 4) * S:(b % 4 + 1) * S],
                                                 xhat[:, b, k * 128:(k + 1) * 128], ident[0:S, 0:S])
                mm.then_inc(s_xt, 1)

            def queries(n):
                pe.wait_ge(s_xts, KC * (n + 1))
                for m in range(KC):
                    if n:
                        pe.wait_ge(s_kt, KC + m + 1)
                    project(bank[4 - 2 * n + m], wq_sb, xhatT, m, 0).then_inc(s_q, 1)

            def values(p):
                if p >= 2:
                    pe.wait_ge(s_vs, p - 1)
                for b in (2 * p, 2 * p + 1):
                    for k in range(KC):
                        mm = nc.tensor.matmul(bank[6 + p % 2][0:S, (b % 2) * D:(b % 2 + 1) * D],
                                              ctxT_sb[:, k, b * S:(b + 1) * S], wv_sb[:, k, :],
                                              start=(k == 0), stop=(k == KC - 1))
                mm.then_inc(s_v, 1)

            pe.wait_ge(s_const, 3)
            keep_clock(4)
            pe.wait_ge(s_wk, 16)
            keys(0)
            pe.wait_ge(s_wv, 16)
            values(0)
            turn_xhat(0)
            values(1)
            pe.wait_ge(s_wq, 16)
            queries(0)

            def scores(b, g, first):
                if g % 2 == 0:
                    pe.wait_ge(s_qn[g // 2], b + 1)
                pe.wait_ge(s_kd[g % 2], 16 * G * (b // 2 + 1))
                if not (first and g < 2):
                    pe.wait_ge(s_mk, NG * b + g - 1)
                nc.tensor.matmul(sc_ps[g % 2], q_now[:, g // 2, :],
                                 k_diag[:, g, :, bass.ds(b % 4, 1), :].rearrange("p h o s -> p h (o s)"),
                                 start=True, stop=True).then_inc(s_sc, 1)

            def turn(b, g, first):
                pe.wait_ge(s_ex, NG * b + g + 1)
                if not (first and g < 2):
                    pe.wait_ge(s_pts, NG * b + g - 1)
                for h in range(G):
                    mm = nc.tensor.transpose(pT_ps[g % 2][:, h, :], probs[:, g, h, :], ident[0:S, 0:S])
                mm.then_inc(s_pt, 1)

            def pv(b, g, first):
                pe.wait_ge(s_pts, NG * b + g + 1)
                if g == 0:
                    pe.wait_ge(s_vp, b + 1)
                    if not first:
                        pe.wait_ge(s_on, b)
                for h in range(G):
                    pair = 2 * g + h // 2
                    at = 32 * (pair % 4)
                    mm = nc.tensor.matmul(oT_ps[at:at + 32, g // 2, :],
                                          v_pad[:, pair, h % 2, :, :].rearrange("p a d -> p (a d)"),
                                          pT_sb[:, g % 2, h, :], start=(h % 2 == 0), stop=(h % 2 == 1))
                mm.then_inc(s_pv, 1)

            def turn_rsum(b, first):
                pe.wait_ge(s_re, b + 1)
                if not first:
                    pe.wait_ge(s_rts, b)
                for k in range(KC):
                    mm = nc.tensor.transpose(rT_ps[:, k, :],
                                             rexp[:, 8 * k:8 * k + 8, :].rearrange("p a d -> p (a d)"),
                                             ident[0:S, 0:S])
                mm.then_inc(s_rt, 1)

            def out_proj(b, first):
                pe.wait_ge(s_on, b + 1)
                if first:
                    pe.wait_ge(s_wo, 16)
                    pe.wait_ge(s_vs, B // 2)
                else:
                    pe.wait_ge(s_yb, b)
                for k in range(KC):
                    mm = nc.tensor.matmul(y_ps, oT_sb[:, k, :], wo_sb[:, k, :], start=(k == 0), stop=(k == KC - 1))
                mm.then_inc(s_y, 1)

            def attend(i, now=True, more=True, last=True, second=False, third=False):
                for g in range(NG):
                    if now and g:
                        scores(i, g, False)
                    if not now and g == 1:
                        keep_clock(4)
                    if last and g == 1:
                        out_proj(i - 2, third)
                    turn(i - 1, g, second)
                    if g:
                        pv(i - 1, g - 1, second)
                turn_rsum(i - 1, second)
                if more:
                    scores(i + 1, 0, False)
                pv(i - 1, NG - 1, second)

            pe.wait_ge(s_kt, KC)
            scores(0, 0, True)
            keys(1)
            pe.wait_ge(s_qt, KC)
            turn_xhat(1)
            scores(0, 1, True)
            scores(0, 2, True)
            queries(1)
            scores(0, 3, True)
            values(2)
            values(3)
            pe.wait_ge(s_qt, 2 * KC)
            scores(1, 0, False)
            attend(1, last=False, second=True)
            attend(2, third=True)
            with pe.Fori(3, B - 1) as i:
                attend(i)
            attend(B - 1, more=False)
            attend(B, now=False, more=False)
            keep_clock(2)
            out_proj(B - 1, False)

            pe.wait_ge(s_pts, NG * B)
            def turn_x2(b):
                pe.wait_ge(s_xh, B + b + 1)
                for k in range(KC):
                    mm = nc.tensor.transpose(bank[2 * (b // 4) + k][:, (b % 4) * S:(b % 4 + 1) * S],
                                             x2n[:, b, k * 128:(k + 1) * 128], ident[0:S, 0:S])
                return mm

            def logits(b):
                pe.wait_ge(s_x2t32, KC * (b // 4 + 1))
                for k in range(KC):
                    mm = nc.tensor.matmul(lg_ps[:, b, :], x2T[:, k, b * S:(b + 1) * S], gw_sb[:, k, :],
                                          start=False, stop=(b == B - 1 and k == KC - 1))
                return mm

            for b in range(4):
                mm = turn_x2(b)
            mm.then_inc(s_x2t, 1)
            keep_clock(2)
            pe.wait_ge(s_gl, 32)
            pe.wait_ge(s_yb, B)
            nc.tensor.matmul(lg_ps, ident[0:1, 0:1].to_broadcast([1, S]),
                             gb_row[:, :].unsqueeze(1).to_broadcast([1, B, ER]), start=True, stop=False)
            for b in range(4):
                logits(b)
            for b in range(4, B):
                mm = turn_x2(b)
            mm.then_inc(s_x2t, 1)
            keep_clock(2)
            for b in range(4, B):
                mm = logits(b)
            mm.then_inc(s_lg, 1)

            SHARED = (E - 1) * PIECES * PW

            def shared_up(n, between=None):
                pe.wait_ge(s_x2lo, 2 * (n + 1))
                for m in range(KC):
                    for half in range(2):
                        if between and m and half:
                            between()
                        if n == 0:
                            pe.wait_ge(s_x2hi, 4)
                        else:
                            pe.wait_ge(s_bb if half else s_aa, m + 1)
                        for k in range(KC):
                            at = SHARED + k * PW + half * F + m * 128
                            terms = ((w_hi, x2T_hi), (w_hi, x2T_lo), (w_lo, x2T_hi))
                            for i, (w, xt) in enumerate(terms):
                                mm = nc.tensor.matmul(bank[2 * m + half][:, 0:HALF], w[:, at:at + 128],
                                                      xt[:, k, n * HALF:(n + 1) * HALF],
                                                      start=(k == 0 and i == 0), stop=(k == KC - 1 and i == 2))
                        mm.then_inc(s_us, 1)

            def count_pairs():
                pe.wait_ge(s_fc, 4)
                pe.wait_ge(s_hot, 1)
                for b in range(B):
                    mm = nc.tensor.matmul(cnt_ps, ones_b[:, :], both[:, B + b, :], start=(b == 0), stop=(b == B - 1))
                mm.then_inc(s_cnt, 1)
                nc.tensor.matmul(pos_ps, before[:, :], both[:, B:, :], start=True, stop=False)
                for back in range(1, B):
                    mm = nc.tensor.matmul(pos_ps, ones_b[:, 0:S], both[:, B - back:2 * B - back, :],
                                          start=False, stop=(back == B - 1))
                mm.then_inc(s_pos, 1)

            pe.wait_ge(s_wlo, PIECES * E)
            shared_up(0, between=count_pairs)
            shared_up(1)
            def shared_down(n):
                pe.wait_ge(s_gsl, 2 * (n + 1))
                for p in (2 * n, 2 * n + 1):
                    if p == 3:
                        pe.wait_ge(s_idx, 1)
                    for b in (2 * p, 2 * p + 1):
                        ps = bank[4 + p][0:S, (b % 2) * D:(b % 2 + 1) * D]
                        t = slice(b * S, (b + 1) * S)
                        for k in range(KC):
                            at = SHARED + KC * PW + k * D
                            terms = ((gs_hi, w_hi), (gs_hi, w_lo), (gs_lo, w_hi))
                            for i, (g, w) in enumerate(terms):
                                mm = nc.tensor.matmul(ps, g[:, k, t], w[:, at:at + D],
                                                      start=(k == 0 and i == 0), stop=(k == KC - 1 and i == 2))
                    mm.then_inc(s_ys, 1)

            pe.wait_ge(s_slot, 1)
            shared_down(0)
            pe.wait_ge(s_tv, 2)
            for kb in range(TOP * B):
                mm = nc.tensor.matmul(map_ps, slot_hot[:, kb, :], tile_val[:, kb, :, :],
                                      start=(kb == 0), stop=(kb == TOP * B - 1))
            mm.then_inc(s_map, 1)
            shared_down(1)

            def split_product(ps, par, sel, parts_hi, parts_lo, col, width, bias_at):
                nc.tensor.matmul(ps, sel[:, par, :].to_broadcast([128, 128]), bias[:, bias_at:bias_at + width],
                                 start=True, stop=False)
                for k in range(KC):
                    rh = w_hi[:, bass.ds(col + k * width, width)]
                    rl = w_lo[:, bass.ds(col + k * width, width)]
                    nc.tensor.matmul(ps, parts_hi[:, par, k, :], rh, start=False, stop=False)
                    nc.tensor.matmul(ps, parts_hi[:, par, k, :], rl, start=False, stop=False)
                    mm = nc.tensor.matmul(ps, parts_lo[:, par, k, :], rh, start=False, stop=(k == KC - 1))
                return mm

            def turn_x(t, n, first):
                par = n % 2
                pe.wait_ge(s_xg[n], (t // XG + 1) * 16)
                if not first:
                    pe.wait_ge(s_xtl, t - 1)
                for k in range(KC):
                    mm = nc.tensor.transpose(xt_ps[par][:, k, :], xg[:, n, k * 128:(k + 1) * 128], ident[:, :])
                mm.then_inc(s_xtp, 1)

            def up(t, par, col, first):
                pe.wait_ge(s_xtl, t + 1)
                if not first:
                    pe.wait_ge(s_gg, t - 1)
                split_product(h_ps[par][:, :], par, sel_up, xT_hi, xT_lo, col, 2 * F, 0).then_inc(s_h, 1)

            def turn_g(t, par, first):
                pe.wait_ge(s_gg, t + 1)
                if not first:
                    pe.wait_ge(s_gtl, t - 1)
                for k in range(2):
                    mm = nc.tensor.transpose(gt_ps[par][:, k, :], gg[:, par, k * 128:(k + 1) * 128], ident[:, :])
                mm.then_inc(s_gt, 1)

            def down(t, par, col, first):
                pe.wait_ge(s_gtl, t + 1)
                if not first:
                    pe.wait_ge(s_yo, t - 1)
                split_product(ye_ps[par][:, 0:D], par, sel_down, gT_hi, gT_lo, col + 2 * PW, D, 2 * F).then_inc(s_ye, 1)

            def column(t):
                return pe.value_load(tile_col[0:1, bass.ds(t, 1)], min_val=0, max_val=(ER - 1) * PIECES * PW)

            def tile_step(t, n, at, first=False, second=False, third=False, more=True):
                par = n % 2
                if more:
                    turn_x(t + 1, (n + 1) % XG, first)
                up(t, par, at[n] if n in at else column(t), first or second)
                if more and n + 1 < XG:
                    at[n + 1] = column(t + 1)
                if second:
                    pe.wait_ge(s_yse, B // 2)
                if not first:
                    turn_g(t - 1, 1 - par, second or third)
                if not (first or second):
                    down(t - 2, par, at[n - 2] if n - 2 in at else column(t - 2), third)

            keep_clock(3, bank[1])
            pe.wait_ge(s_bias, 32)
            pe.wait_ge(s_te, 2)
            turn_x(0, 0, True)
            keep_clock(1, bank[1])
            at = {0: column(0)}
            tile_step(0, 0, at, first=True)
            tile_step(1, 1, at, second=True)
            tile_step(2, 2, at, third=True)
            tile_step(3, 3, at)
            with pe.Fori(XG, NT - 1, XG) as t:
                at = {0: column(t)}
                for n in range(XG):
                    tile_step(t + n, n, at)
            at = {0: column(NT - 1)}
            tile_step(NT - 1, 0, at, more=False)
            turn_g(NT - 1, 0, False)
            down(NT - 2, 1, column(NT - 2), False)
            down(NT - 1, 0, at[0], False)

        @block.scalar
        def _(act):
            act.dma_start(wk_sb[:, :, :], wkT).then_inc(s_wk, 16)
            act.dma_start(wq_sb[:, :, :], wqT).then_inc(s_wq, 16)
            nc.scalar.preload_act_table(ACT.Sqrt)

            def root(lo, hi, nth):
                act.wait_ge(s_stats, nth)
                nc.scalar.activation(std[:, lo:hi], std[:, lo:hi], ACT.Sqrt).then_inc(s_std, 1)

            root(0, B // 2, 1)
            act.wait_ge(s_bqk, 16)

            def take_keys(n):
                for m in range(KC):
                    act.wait_ge(s_k, 2 * n + m + 1)
                    nc.scalar.activation(kT[:, m, n * HALF:(n + 1) * HALF], bank[2 * n + m][:, 0:HALF], ACT.Identity,
                                         bias=bqk_sb[:, 1, m:m + 1]).then_inc(s_kt, 1)

            def take_xhatT(n):
                act.wait_ge(s_xt, n + 1)
                if n:
                    act.wait_ge(s_q, KC)
                for k in range(KC):
                    nc.scalar.activation(xhatT[:, k, :], bank[2 * n + 2 + k][:, 0:HALF],
                                         ACT.Copy).then_inc(s_xts, 1)

            def take_queries(b, k, first=False):
                if not first:
                    act.wait_ge(s_sc, NG * (b - 1) + 2 * k + 2)
                nc.scalar.activation(q_now[:, k, :], qT[:, k, bass.ds(b * S, S)], ACT.Copy).then_inc(s_qn[k], 1)

            def take_qT(n):
                for m in range(KC):
                    if n == 0 and m:
                        act.wait_ge(s_qt, 1)
                        take_queries(0, 0, first=True)
                    act.wait_ge(s_q, 2 * n + m + 1)
                    nc.scalar.activation(qT[:, m, n * HALF:(n + 1) * HALF], bank[4 - 2 * n + m][:, 0:HALF],
                                         ACT.Identity, bias=bqk_sb[:, 0, m:m + 1]).then_inc(s_qt, 1)

            def take_values(b):
                for par in range(2):
                    ins = nc.scalar.activation(
                        v_pad[:, :, par, par, :],
                        v_sb[:, bass.ds(b, 1), :].rearrange("p o (a q d) -> p (o a) q d", q=2, d=HD)[:, :, par, :],
                        ACT.Copy)
                ins.then_inc(s_vp, 1)

            def exps(b, g, first):
                act.wait_ge(s_sh, NG * b + g + 1)
                if not first:
                    act.wait_ge(s_pt, NG * (b - 1) + g + 1)
                    act.wait_ge(s_sum, NG * (b - 1) + g + 1)
                nc.scalar.activation(probs[:, g, :, :], sc_sb[:, g % 2, :, :], ACT.Exp, scale=HD ** -0.5)\
                    .then_inc(s_ex, 1)

            def take_pT(b, g, first):
                act.wait_ge(s_pt, NG * b + g + 1)
                if not (first and g < 2):
                    act.wait_ge(s_pv, NG * b + g - 1)
                nc.scalar.activation(pT_sb[:, g % 2, :, :], pT_ps[g % 2], ACT.Copy).then_inc(s_pts, 1)

            def round_weights(e, j):
                act.wait_ge(s_raw[j], 16 * (e + 1))
                nc.scalar.activation(w_hi[:, bass.ds(PW * (PIECES * e + j), PW)], raw[:, j, :], ACT.Copy)\
                    .then_inc(s_whi, 1)

            def take_rT(b, first):
                act.wait_ge(s_rt, b + 1)
                if not first:
                    act.wait_ge(s_on, b)
                nc.scalar.activation(rT_sb[:, :, :], rT_ps, ACT.Copy).then_inc(s_rts, 1)

            def attend(i, now=True, before=True, more=True, first=False, second=False):
                for g in range(NG):
                    if before:
                        take_pT(i - 1, g, second)
                    if g == NG - 1 and before:
                        take_rT(i - 1, second)
                    if g == 0 and before:
                        exps(i - 1, NG - 1, second)
                    if g and now:
                        exps(i, g - 1, first)
                    if g >= 2 and more:
                        take_queries(i + 1, g - 2)
                    if g < PIECES:
                        round_weights(i, g)
                if before:
                    act.wait_ge(s_pv, NG * i)
                if now:
                    take_values(i)

            take_keys(0)
            root(B // 2, B, 2)
            take_xhatT(0)
            act.wait_ge(s_gates, 16)
            nc.scalar.activation(tanh_gate[:, :], gate_cols[:, :], ACT.Tanh).then_inc(s_tg, 1)
            take_qT(0)
            act.wait_ge(s_qt, KC)
            take_queries(0, 1, first=True)
            take_keys(1)
            take_xhatT(1)
            exps(0, 0, True)
            round_weights(0, 0)
            exps(0, 1, True)
            round_weights(0, 1)
            take_queries(1, 0)
            take_qT(1)
            exps(0, 2, True)
            round_weights(0, 2)
            take_queries(1, 1)
            act.wait_ge(s_vs, B // 2)
            act.wait_ge(s_const, 5)
            act.wait_ge(s_qt, 2 * KC)
            take_values(0)
            attend(1, second=True)
            with act.Fori(2, B - 1) as i:
                attend(i)
            attend(B - 1, more=False)
            attend(B, now=False, more=False)

            nc.scalar.preload_act_table(ACT.Sqrt)
            root(0, B - 1, 3)

            def take_x2T(n):
                act.wait_ge(s_x2t, n + 1)
                for k in range(KC):
                    src, at = bank[2 * n + k][:, 0:HALF], slice(n * HALF, (n + 1) * HALF)
                    nc.scalar.activation(x2T[:, k, at], src, ACT.Copy).then_inc(s_x2t32, 1)

            def round_x2T(n):
                for k in range(KC):
                    src, at = bank[2 * n + k][:, 0:HALF], slice(n * HALF, (n + 1) * HALF)
                    nc.scalar.activation(x2T_hi[:, k, at], src, ACT.Copy).then_inc(s_x2hi, 1)

            take_x2T(0)
            root(B - 1, B, 4)
            round_x2T(0)
            take_x2T(1)
            nc.scalar.preload_act_table(ACT.Exp)
            round_x2T(1)
            act.wait_ge(s_b, 48)
            nc.scalar.activation(b1s_half[:, :], b1s[:, 0:KC], ACT.Copy, scale=0.5).then_inc(s_tha, 1)
            act.wait_ge(s_gexp, 1)
            nc.scalar.activation(pg[:, :, :], pg[:, :, :], ACT.Exp).then_inc(s_gexp, 1)
            act.wait_ge(s_tha, 1)
            def shared_parts(t):
                m, a, b, u = t % 2, a_sh[t % 2], b_sh[t % 2], u_sh[t % 2]
                act.wait_ge(s_us, 2 * t + 1)
                if t == 1:
                    act.wait_ge(s_xr, 32)
                if t >= 2:
                    act.wait_ge(s_gs, t - 1)
                nc.scalar.activation(b, bank[2 * m][:, 0:HALF], ACT.Tanh, bias=b1s_half[:, m:m + 1],
                                     scale=0.5).then_inc(s_tha, 1)
                nc.scalar.activation(a, bank[2 * m][:, 0:HALF], ACT.Identity, bias=b1s_half[:, m:m + 1],
                                     scale=0.5)
                act.wait_ge(s_tha, t + 2)
                nc.scalar.activation(u, b, ACT.Copy, bias=1.0).then_inc(s_aa, 1)
                act.wait_ge(s_us, 2 * t + 2)
                act.wait_ge(s_aa, t + 1)
                nc.scalar.activation(b, bank[2 * m + 1][:, 0:HALF], ACT.Identity,
                                     bias=b1s[:, KC + m:KC + m + 1]).then_inc(s_bb, 1)

            def shared_high(t):
                m, at = t % 2, slice(t // 2 * HALF, (t // 2 + 1) * HALF)
                act.wait_ge(s_gs, t + 1)
                nc.scalar.activation(gs_hi[:, m, at], g_sh[:, m, at], ACT.Copy).then_inc(s_gsh, 1)

            shared_parts(0)
            for t in range(1, 4):
                shared_parts(t)
                shared_high(t - 1)
            shared_high(3)

            def take_x(t, par, first):
                act.wait_ge(s_xtp, t + 1)
                if not first:
                    act.wait_ge(s_h, t - 1)
                nc.scalar.activation(xT_hi[:, par, :, :], xt_ps[par], ACT.Copy).then_inc(s_xth, 1)

            def tanh_a(t, par, first):
                act.wait_ge(s_h, t + 1)
                if not first:
                    act.wait_ge(s_ug, t - 1)
                nc.scalar.activation(th[:, par, :], h_ps[par][:, 0:F], ACT.Tanh, scale=0.5).then_inc(s_th, 1)

            def take_g(t, par, first):
                act.wait_ge(s_gt, t + 1)
                if not first:
                    act.wait_ge(s_ye, t - 1)
                nc.scalar.activation(gT_hi[:, par, :, :], gt_ps[par], ACT.Copy).then_inc(s_gth, 1)

            def weigh(t, par, first):
                act.wait_ge(s_ye, t + 1)
                if not first:
                    act.wait_ge(s_yw[par], (t // 2) * 16)
                nc.scalar.activation(ye[:, par, :], ye_ps[par][:, 0:D], ACT.Copy, scale=slot_w[:, bass.ds(t, 1)])\
                    .then_inc(s_yo, 1)

            def tile_step(t, par, first=False, second=False, third=False, fourth=False, more=True, now=True):
                if now:
                    if more:
                        take_x(t + 1, 1 - par, first)
                    tanh_a(t, par, first or second)
                if not first:
                    take_g(t - 1, 1 - par, second or third)
                if not (first or second):
                    weigh(t - 2, par, third or fourth)

            act.wait_ge(s_idx, 1)
            act.wait_ge(s_sw, 1)
            act.wait_ge(s_bias, 32)
            take_x(0, 0, True)
            tile_step(0, 0, first=True)
            tile_step(1, 1, second=True)
            tile_step(2, 0, third=True)
            tile_step(3, 1, fourth=True)
            with act.Fori(4, NT - 1, 2) as t:
                tile_step(t, 0)
                tile_step(t + 1, 1)
            tile_step(NT - 1, 0, more=False)
            tile_step(NT, 1, now=False)
            weigh(NT - 1, 0, False)

        @block.vector
        def _(dve):
            def variances(lo, hi, before):
                for b in range(lo, hi):
                    dve.wait_ge(s_st, before + b - lo + 1)
                    nc.vector.bn_aggr(meanvar[:, b, :], stats[:, b, :]).then_inc(s_st2, 1)
                dve.wait_ge(s_st2, before + hi - lo)
                nc.vector.tensor_scalar(std[:, lo:hi], meanvar[:, lo:hi, 1], EPS, None, ALU.add).then_inc(s_stats, 1)

            def inverses(lo, hi, nth):
                dve.wait_ge(s_std, nth)
                nc.vector.reciprocal(rstd[:, lo:hi], std[:, lo:hi]).then_inc(s_rstd, 1)
                dve.wait_ge(s_rstd, nth)

            def scale(src, dst, lo, hi):
                for b in range(lo, hi):
                    nc.vector.tensor_scalar(dst[:, b, :], src[:, b, :], meanvar[:, b, 0:1], rstd[:, b:b + 1],
                                            ALU.subtract, ALU.mult).then_inc(s_xh, 1)

            for n in range(2):
                lo, hi = n * B // 2, (n + 1) * B // 2
                dve.wait_ge(s_x[n], 16)
                for b in range(lo, hi):
                    nc.vector.bn_stats(stats[:, b, :], x_sb[:, b, :]).then_inc(s_st, 1)
                variances(lo, hi, lo)
                inverses(lo, hi, n + 1)
                scale(x_sb, xhat, lo, hi)
            dve.wait_ge(s_bvo, 16)
            dve.wait_ge(s_xt, 1)

            def add_bv(p):
                dve.wait_ge(s_v, p + 1)
                nc.vector.tensor_tensor(v_sb[:, 2 * p:2 * p + 2, :], grid(bank[6 + p % 2], S, 2, D),
                                        bvo_sb[:, 0:1, :].to_broadcast([S, 2, D]), ALU.add).then_inc(s_vs, 1)

            def mask_scores(g):
                for h in range(G):
                    ins = nc.vector.tensor_tensor_reduce(
                        out=sc_sb[:, g % 2, h, :], in0=sc_ps[g % 2][:, h, :], in1=mask[:, :], scale=1.0,
                        scalar=LEAST, op0=ALU.add, op1=ALU.max, accum_out=rowmax[:, g % 2, h:h + 1])
                ins.then_inc(s_mk, 1)

            def sum_probs(b, g):
                dve.wait_ge(s_ex, NG * b + g + 1)
                nc.vector.tensor_reduce(sums[:, G * g:G * g + G], probs[:, g, :, :], AX.X, ALU.add)\
                    .then_inc(s_sum, 1)

            def recip_sums(b, first):
                dve.wait_ge(s_sum, NG * (b + 1))
                nc.vector.reciprocal(rsum[:, :], sums[:, :]).then_inc(s_rs, 1)

            def spread_sums(b, first):
                dve.wait_ge(s_rs, b + 1)
                if not first:
                    dve.wait_ge(s_rt, b)
                nc.vector.tensor_copy(rexp[:, :, :], rsum[:, :].unsqueeze(2).to_broadcast([S, HEADS, HD]))\
                    .then_inc(s_re, 1)

            def norm_outputs(b, first):
                dve.wait_ge(s_rts, b + 1)
                dve.wait_ge(s_pv, NG * (b + 1))
                if not first:
                    dve.wait_ge(s_y, b)
                nc.vector.tensor_tensor(oT_sb[:, :, :], oT_ps, rT_sb[:, :, :], ALU.mult).then_inc(s_on, 1)

            def add_bo(b):
                dve.wait_ge(s_y, b + 1)
                nc.vector.tensor_tensor(y_sb[:, :], y_ps, bvo_sb[:, 1, :], ALU.add).then_inc(s_yb, 1)

            def residual(b):
                dve.wait_ge(s_yb, b + 1)
                xb = x_sb[:, bass.ds(b, 1), :].rearrange("p o d -> p (o d)")
                nc.vector.scalar_tensor_tensor(out=xb, in0=y_sb[:, :], scalar=tanh_gate[0:S, 0:1], in1=xb,
                                               op0=ALU.mult, op1=ALU.add).then_inc(s_x2, 1)

            def take_stats(b):
                at = bass.ds(b, 1)
                dve.wait_ge(s_x2, b + 1)
                nc.vector.bn_stats(stats[:, at, :].rearrange("p o d -> p (o d)"),
                                   x_sb[:, at, :].rearrange("p o d -> p (o d)")).then_inc(s_st, 1)

            def attend(i, now=True, before=True, last=True, first=False, second=False):
                for g in range(NG):
                    if now:
                        dve.wait_ge(s_sc, NG * i + g + 1)
                    if g == 2 and before:
                        spread_sums(i - 1, second)
                    if now and g >= 2:
                        sum_probs(i, g - 2)
                    elif before and g < 2:
                        sum_probs(i - 1, g + 2)
                    if now:
                        mask_scores(g)
                    if g == 1 and before:
                        recip_sums(i - 1, second)
                    if g == 2 and last:
                        add_bo(i - 2)
                    if g == 3 and last:
                        residual(i - 2)
                if now and before:
                    norm_outputs(i - 1, second)
                if last:
                    take_stats(i - 2)

            dve.wait_ge(s_tg, 1)
            dve.wait_ge(s_const, 4)
            add_bv(0)
            add_bv(1)
            for g in range(NG):
                dve.wait_ge(s_sc, g + 1)
                if g >= 2:
                    sum_probs(0, g - 2)
                mask_scores(g)
            add_bv(2)
            add_bv(3)
            attend(1, last=False, second=True)
            with dve.Fori(2, B) as i:
                attend(i)
            attend(B, now=False)
            variances(0, B - 1, B)
            norm_outputs(B - 1, False)
            inverses(0, B - 1, 3)
            scale(x_sb, x2n, 0, 4)
            add_bo(B - 1)
            residual(B - 1)
            take_stats(B - 1)
            variances(B - 1, B, 2 * B - 1)
            scale(x_sb, x2n, 4, B - 1)
            inverses(B - 1, B, 4)
            scale(x_sb, x2n, B - 1, B)
            dve.wait_ge(s_b, 48)
            nc.vector.tensor_copy(b_hi[:, :], b_raw[:, :]).then_inc(s_brow, 1)
            dve.wait_ge(s_brow, 1)
            nc.vector.tensor_tensor(b_lo[:, :], b_raw[:, :], b_hi[:, :], ALU.subtract).then_inc(s_brow, 1)

            steps = [0]

            def step(ins):
                steps[0] += 1
                ins.then_inc(s_chain, 1)
                dve.wait_ge(s_chain, steps[0])

            def over_e(t):
                return t.unsqueeze(2).to_broadcast([S, B, ER])

            dve.wait_ge(s_fc, 4)
            step(nc.vector.tensor_scalar(late[:, 0:1], row8[:, :], ER - 0.5, -float(ER), ALU.is_ge, ALU.mult))
            step(nc.vector.tensor_tensor(row8[:, :], row8[:, :], late[:, 0:1], ALU.add))
            dve.wait_ge(s_lg, 1)
            step(nc.vector.tensor_reduce(gsum[:, :], lg_ps, AX.X, ALU.max))
            nc.vector.tensor_tensor(pg[:, :, :], lg_ps, over_e(gsum[:, :]), ALU.subtract).then_inc(s_gexp, 1)
            dve.wait_ge(s_gexp, 2)
            step(nc.vector.scalar_tensor_tensor(out=eq[:, :, :], in0=pg[:, :, :], scalar=1.0, in1=rank[:, :, :],
                                                op0=ALU.is_equal, op1=ALU.mult))
            step(nc.vector.tensor_reduce(first[:, :], eq[:, :, :], AX.X, ALU.min))
            step(nc.vector.tensor_tensor(hot[:, 0, :, :], eq[:, :, :], over_e(first[:, :]), ALU.is_equal))
            step(nc.vector.scalar_tensor_tensor(out=pg2[:, :, :], in0=hot[:, 0, :, :], scalar=-4.0,
                                                in1=pg[:, :, :], op0=ALU.mult, op1=ALU.add))
            step(nc.vector.tensor_reduce(top[:, 1, :], pg2[:, :, :], AX.X, ALU.max))
            step(nc.vector.tensor_tensor(eq[:, :, :], pg2[:, :, :], over_e(top[:, 1, :]), ALU.is_equal))
            step(nc.vector.tensor_tensor(eq[:, :, :], eq[:, :, :], rank[:, :, :], ALU.mult))
            step(nc.vector.tensor_reduce(first[:, :], eq[:, :, :], AX.X, ALU.min))
            step(nc.vector.tensor_tensor(hot[:, 1, :, :], eq[:, :, :], over_e(first[:, :]), ALU.is_equal))
            nc.vector.tensor_tensor(both[:, B:, :], hot[:, 0, :, :], hot[:, 1, :, :], ALU.add).then_inc(s_hot, 1)
            step(nc.vector.tensor_reduce(gsum[:, :], pg[:, :, :], AX.X, ALU.add))
            step(nc.vector.reciprocal(top[:, 0, :], gsum[:, :]))
            step(nc.vector.tensor_tensor(top[:, 1, :], top[:, 1, :], top[:, 0, :], ALU.mult))
            KB = TOP * B
            top16 = top[:, :, :].rearrange("p k b -> p (k b)")
            step(nc.vector.tensor_copy(top_hi[:, :], top16))
            nc.vector.tensor_copy(vals[:, :, 2], top_hi[:, :].bitcast(F32))
            nc.vector.tensor_tensor(vals[:, :, 3], top16, top_hi[:, :].bitcast(F32), ALU.subtract)
            def shared_low(t):
                m, at = t % 2, slice(t // 2 * HALF, (t // 2 + 1) * HALF)
                dve.wait_ge(s_gsh, t + 1)
                nc.vector.tensor_tensor(gs_lo[:, m, at], g_sh[:, m, at], gs_hi[:, m, at], ALU.subtract)\
                    .then_inc(s_gsl, 1)

            dve.wait_ge(s_cnt, 1)
            step(nc.vector.tensor_tensor(cnt_gt[:, :, :], iota_j[:, :, :],
                                         cnt_ps.unsqueeze(2).to_broadcast([128, ER, 7]), ALU.is_lt))
            step(nc.vector.tensor_reduce(tiles[:, :], cnt_gt[:, :, :], AX.X, ALU.add))
            step(nc.vector.tensor_tensor(t_less[:, :, :], less[:, :, :],
                                         tiles[:, :].unsqueeze(1).to_broadcast([128, ER, ER]), ALU.mult))
            step(nc.vector.tensor_reduce(tile0[:, :], t_less[:, :, :], AX.X, ALU.add))
            dve.wait_ge(s_pos, 1)
            step(nc.vector.scalar_tensor_tensor(out=slots[:, :, :],
                                                in0=tile0[0:S, :].unsqueeze(1).to_broadcast([S, B, ER]),
                                                scalar=float(PART), in1=pos_ps, op0=ALU.mult, op1=ALU.add))
            for k in range(TOP):
                last = nc.vector.tensor_tensor(slot_e[:, k, :, :], hot[:, k, :, :], slots[:, :, :], ALU.mult)
            step(last)
            nc.vector.tensor_reduce(slot[:, :], slot_e[:, :, :, :].rearrange("p k b e -> p (k b) e"), AX.X, ALU.add)\
                .then_inc(s_slot, 1)
            dve.wait_ge(s_slot, 1)
            step(nc.vector.tensor_scalar(slot_ti[:, :], slot[:, :], PART / 2 - 0.5, 1.0 / PART, ALU.subtract, ALU.mult))
            step(nc.vector.tensor_copy(slot_t[:, :], slot_ti[:, :]))
            step(nc.vector.scalar_tensor_tensor(out=slot_p[:, :], in0=slot_t[:, :], scalar=-float(PART),
                                                in1=slot[:, :], op0=ALU.mult, op1=ALU.add))
            step(nc.vector.tensor_tensor(eq_t[:, :, :], iota_tok[:, :].unsqueeze(1).to_broadcast([S, KB, NT]),
                                         slot_t[:, :].unsqueeze(2).to_broadcast([S, KB, NT]), ALU.is_equal))
            nc.vector.tensor_tensor(tile_val[:, :, :, :], eq_t[:, :, :].unsqueeze(2).to_broadcast([S, KB, NV, NT]),
                                    vals[:, :, :].unsqueeze(3).to_broadcast([S, KB, NV, NT]), ALU.mult).then_inc(s_tv, 1)
            shared_low(0)
            shared_low(1)
            nc.vector.tensor_tensor(slot_hot[:, :, :], iota_p[:, :].unsqueeze(1).to_broadcast([S, KB, PART]),
                                    slot_p[:, :].unsqueeze(2).to_broadcast([S, KB, PART]), ALU.is_equal).then_inc(s_tv, 1)
            step(nc.vector.tensor_tensor(t_ge[:, :, :], iota_t[:, :, :],
                                         tile0[:, :].unsqueeze(1).to_broadcast([128, NT, ER]), ALU.is_ge))
            step(nc.vector.tensor_reduce(tile_e[:, :], t_ge[:, :, :], AX.X, ALU.add))
            step(nc.vector.tensor_scalar(tile_e[:, :], tile_e[:, :], -1.0, None, ALU.add))
            nc.vector.tensor_scalar(tile_col[0:1, 0:NT], tile_e[0:1, :], float(PIECES * PW), None, ALU.mult).then_inc(s_te, 1)
            nc.vector.tensor_scalar(e_hot[:, 0:NT], tile_e[:, :], row8[:, 0:1], None, ALU.is_equal).then_inc(s_te, 1)
            shared_low(2)
            shared_low(3)
            dve.wait_ge(s_map, 1)
            step(nc.vector.tensor_copy(smap[:, :, :], map_ps))
            nc.vector.tensor_scalar(late[:, :], smap[:, 1, :], TOK - 0.5, -float(TOK), ALU.is_ge, ALU.mult)
            step(nc.vector.scalar_tensor_tensor(out=empty[:, :], in0=smap[:, 0, :], scalar=1.0, in1=dump[:, :],
                                                op0=ALU.subtract, op1=ALU.mult))
            nc.vector.tensor_tensor(tok_i[:, 0:NT], late[:, :], smap[:, 1, :], ALU.add)
            nc.vector.tensor_tensor(row_i[:, 0:NT], empty[:, :], smap[:, 1, :], ALU.add).then_inc(s_idx, 1)
            step(nc.vector.tensor_tensor(slot_w[:, 0:NT], smap[:, 2, :], smap[:, 3, :], ALU.add))
            nc.vector.tensor_scalar(slot_w[:, 0:NT], slot_w[:, 0:NT], tanh_gate[:, 1:2], None, ALU.mult)\
                .then_inc(s_sw, 1)

            dve.wait_ge(s_xr, 32)
            for p in range(B // 2):
                dve.wait_ge(s_ys, p + 1)
                nc.vector.tensor_tensor(acc[:, 2 * p:2 * p + 2, :], grid(bank[4 + p], S, 2, D),
                                        b2s[:, :].unsqueeze(1).to_broadcast([S, 2, D]), ALU.add).then_inc(s_yse, 1)

            dve.wait_ge(s_yse, B // 2)

            def add_shared(b):
                at = bass.ds(b * D, D)
                nc.vector.scalar_tensor_tensor(out=x_flat[:, at], in0=x2n_all[0:S, at], scalar=tanh_gate[0:S, 1:2],
                                               in1=x_flat[:, at], op0=ALU.mult, op1=ALU.add).then_inc(s_xs, 1)

            def take_x(t, par, first):
                if not first:
                    dve.wait_ge(s_h, t - 1)
                nc.vector.tensor_copy(sel_up[:, par, :], e_hot[:, bass.ds(t, 1)])
                dve.wait_ge(s_xth, t + 1)
                nc.vector.tensor_tensor(xT_lo[:, par, :, :], xt_ps[par], xT_hi[:, par, :, :], ALU.subtract)\
                    .then_inc(s_xtl, 1)

            def gate(t, par, first):
                dve.wait_ge(s_th, t + 1)
                nc.vector.scalar_tensor_tensor(out=ug[:, par, :], in0=th[:, par, :], scalar=1.0,
                                               in1=h_ps[par][:, 0:F], op0=ALU.add, op1=ALU.mult).then_inc(s_ug, 1)
                dve.wait_ge(s_ug, t + 1)
                if not first:
                    dve.wait_ge(s_gt, t - 1)
                nc.vector.scalar_tensor_tensor(out=gg[:, par, :], in0=ug[:, par, :], scalar=0.5,
                                               in1=h_ps[par][:, F:2 * F], op0=ALU.mult, op1=ALU.mult).then_inc(s_gg, 1)

            def take_g(t, par, first=False):
                if not first:
                    dve.wait_ge(s_ye, t - 1)
                nc.vector.tensor_copy(sel_down[:, par, :], e_hot[:, bass.ds(t, 1)])
                dve.wait_ge(s_gth, t + 1)
                nc.vector.tensor_tensor(gT_lo[:, par, :, :], gt_ps[par], gT_hi[:, par, :, :], ALU.subtract)\
                    .then_inc(s_gtl, 1)

            def tile_step(t, par, first=False, second=False, third=False, more=True):
                if more:
                    take_x(t + 1, 1 - par, first)
                gate(t, par, first or second)
                if not first:
                    take_g(t - 1, 1 - par, second or third)

            dve.wait_ge(s_bias, 32)
            take_x(0, 0, True)
            tile_step(0, 0, first=True)
            tile_step(1, 1, second=True)
            tile_step(2, 0, third=True)
            tile_step(3, 1)
            assert (NT - 5) // 2 == B
            with dve.Fori(4, NT - 1, 2) as t:
                tile_step(t, 0)
                tile_step(t + 1, 1)
                add_shared(t // 2 - 2)
            tile_step(NT - 1, 0, more=False)
            take_g(NT - 1, 0)
            dve.wait_ge(s_xs, B)
            for n, b in enumerate(b for b in range(B) if b not in POOL_SUMS):
                dve.wait_ge(s_yback[b], 16)
                nc.vector.tensor_tensor(acc[:, b, :], y_back[:, 0, b, :], y_back[:, 1, b, :], ALU.add)\
                    .then_inc(s_rsum, 1)
                dve.wait_ge(s_rsum, n + 1)
                nc.vector.tensor_tensor(acc[:, b, :], acc[:, b, :], x_sb[:, b, :], ALU.add).then_inc(s_fin[b], 1)


def kernel(**inputs):
    import numpy as np
    import concourse.bacc as bacc
    from concourse.bass_utils import run_bass_kernel_spmd

    def rows(a):
        return np.ascontiguousarray(a.reshape(KC, 128, -1).transpose(1, 0, 2))

    a = {k: np.asarray(v) for k, v in inputs.items()}
    w1 = np.concatenate([a["L0_ffn_rw1"], a["L0_ffn_sw1"]])
    w2 = np.concatenate([a["L0_ffn_rw2"], a["L0_ffn_sw2"]])
    w1 = w1.reshape(E, KC, 128, 2 * F)
    w2 = w2.reshape(E, 1, KC, 128, D).transpose(0, 1, 3, 2, 4).reshape(E, 1, 128, KC * D)
    ctx = a["ctx_1024"][:, :S, :].transpose(2, 0, 1).reshape(D, TOK)
    arrays = {
        "x": np.ascontiguousarray(a["x"].transpose(1, 0, 2)),
        "ctxT": rows(ctx),
        "wqT": rows(a["L0_xattn_Wq"].T), "wkT": rows(a["L0_xattn_Wk"].T),
        "wvT": rows(a["L0_xattn_Wv"].T), "woT": rows(a["L0_xattn_Wo"].T),
        "bqk": np.ascontiguousarray(np.stack([a["L0_xattn_bq"], a["L0_xattn_bk"]]).reshape(2, KC, 128).transpose(2, 0, 1)),
        "bvo": np.stack([a["L0_xattn_bv"], a["L0_xattn_bo"]]),
        "gates": np.concatenate([a["g_xattn"], a["g_ffn"]]),
        "gate_w": rows(a["L0_ffn_gate_w"]),
        "gate_b": a["L0_ffn_gate_b"].reshape(1, ER),
        "w_all": np.ascontiguousarray(np.concatenate([w1, w2], axis=1).reshape(E * PIECES, 128, PW)),
        "b_routed": np.ascontiguousarray(np.concatenate([a["L0_ffn_rb1"], a["L0_ffn_rb2"]], axis=1)),
        "b1_shared": np.ascontiguousarray(a["L0_ffn_sb1"].reshape(2 * KC, 128).T),
        "b2_shared": a["L0_ffn_sb2"].reshape(D),
    }
    nc = bacc.Bacc("TRN2", target_bir_lowering=False, num_devices=1)
    aps = [nc.dram_tensor(f"in_{n}", v.shape, F32, kind="ExternalInput").ap() for n, v in arrays.items()]
    out = nc.dram_tensor("out", (B, S, D), F32, kind="ExternalOutput").ap()
    block_kernel(nc, *aps, out)
    r = run_bass_kernel_spmd(nc, [{f"in_{n}": v for n, v in arrays.items()}], core_ids=[0])
    return r.results[0]["out"]
```
